# Optimizing a Trainium2 kernel written in Bass

```python
import numpy as np
import jax
import jax.numpy as jnp

def _softmax(x, axis=-1):
    return jax.nn.softmax(x, axis=axis)

def _gelu(x):
    return jax.nn.gelu(x, approximate=True)

def _silu(x):
    return jax.nn.silu(x)

def _sigmoid(x):
    return jax.nn.sigmoid(x)

def _layernorm(x, axis=-1, eps=1e-05):
    m = jnp.mean(x, axis=axis, keepdims=True)
    v = jnp.var(x, axis=axis, keepdims=True)
    return (x - m) / jnp.sqrt(v + eps)

def _scatter_add(tgt, idx, src, axis=0):
    return tgt.at[idx].add(src)

def _segment_sum(src, seg, n):
    return jax.ops.segment_sum(src, seg, n)
kernel_name = 'mk_hybrid_d1_jaxref_r4_ed40ea'

def setup_inputs(seed: int=0):
    np.random.seed(seed)
    _w = jnp.asarray

    def _L0_attn_a_setup():
        import jax, jax.numpy as jnp
        import numpy as np
        B, T, C = (8, 256, 512)

        def wkv(time_decay, time_first, k, v):
            w = -jnp.exp(time_decay)
            u = time_first
            b, t, c = k.shape
            k_t = jnp.transpose(k, (1, 0, 2))
            v_t = jnp.transpose(v, (1, 0, 2))

            def step(carry, kv):
                p, q, o = carry
                kt, vt = kv
                no = jnp.maximum(o, u + kt)
                A = jnp.exp(o - no)
                Bc = jnp.exp(u + kt - no)
                y = (A * p + Bc * vt) / (A * q + Bc)
                no2 = jnp.maximum(w + o, kt)
                A2 = jnp.exp(w + o - no2)
                B2 = jnp.exp(kt - no2)
                return ((A2 * p + B2 * vt, A2 * q + B2, no2), y)
            init = (jnp.zeros((b, c), k.dtype), jnp.zeros((b, c), k.dtype), jnp.full((b, c), -1e+38, k.dtype))
            _, y = jax.lax.scan(step, init, (k_t, v_t))
            return jnp.transpose(y, (1, 0, 2))
        key = jax.random.key(seed)
        k1, k2, k3, k4, k5 = jax.random.split(key, 5)
        x = jax.random.normal(k1, (B, T, C), dtype=jnp.float32)
        W_rvk = jax.random.normal(k2, (3 * C, C), dtype=jnp.float32) / np.sqrt(C).astype(np.float32)
        W_out = jax.random.normal(k3, (C, C), dtype=jnp.float32) / np.sqrt(C).astype(np.float32)
        time_decay = jax.random.normal(k4, (C,), dtype=jnp.float32) * 0.1
        time_first = jax.random.normal(k5, (C,), dtype=jnp.float32) * 0.1
        return {'x': x, 'W_rvk': W_rvk, 'W_out': W_out, 'time_decay': time_decay, 'time_first': time_first}
    _L0_attn_a_in = _L0_attn_a_setup()

    def _L0_attn_b_setup():
        import jax, jax.numpy as jnp
        import numpy as np
        HIDDEN = 512
        INTER = 1024
        STATE = 16
        KCONV = 4
        DT_RANK = 128
        B_SZ = 2
        L_SEQ = 512

        def _mamba_forward(hidden_states, in_proj_w, conv_w, conv_b, x_proj_w, dt_proj_w, dt_proj_b, A_log, D_param, out_proj_w):
            Bsz, L, _ = hidden_states.shape
            proj = jnp.einsum('blh,eh->ble', hidden_states, in_proj_w)
            x, gate = (proj[..., :INTER], proj[..., INTER:])
            xc = jnp.swapaxes(x, 1, 2)
            xc = jax.lax.conv_general_dilated(xc, conv_w, window_strides=(1,), padding=[(KCONV - 1, 0)], dimension_numbers=('NCH', 'OIH', 'NCH'), feature_group_count=INTER)
            xc = jax.nn.silu(xc + conv_b[None, :, None])
            u = jnp.swapaxes(xc, 1, 2)
            ssm_p = jnp.einsum('bld,rd->blr', u, x_proj_w)
            dt_lr = ssm_p[..., :DT_RANK]
            Bm = ssm_p[..., DT_RANK:DT_RANK + STATE]
            Cm = ssm_p[..., DT_RANK + STATE:]
            delta = jax.nn.softplus(jnp.einsum('blr,dr->bld', dt_lr, dt_proj_w) + dt_proj_b)
            A = -jnp.exp(A_log)

            def step(h, xs):
                d_t, B_t, C_t, u_t = xs
                dA = jnp.exp(d_t[..., None] * A)
                h = h * dA + (d_t * u_t)[..., None] * B_t[:, None, :]
                y_t = jnp.einsum('bdn,bn->bd', h, C_t)
                return (h, y_t)
            h0 = jnp.zeros((Bsz, INTER, STATE), delta.dtype)
            xs = (jnp.moveaxis(delta, 1, 0), jnp.moveaxis(Bm, 1, 0), jnp.moveaxis(Cm, 1, 0), jnp.moveaxis(u, 1, 0))
            _, ys = jax.lax.scan(step, h0, xs)
            y = jnp.moveaxis(ys, 0, 1) + u * D_param
            y = y * jax.nn.silu(gate)
            return jnp.einsum('bld,hd->blh', y, out_proj_w)
        key = jax.random.key(seed)
        ks = jax.random.split(key, 10)
        s = lambda fan: 1.0 / np.sqrt(fan)
        inp = {'hidden_states': jax.random.normal(ks[0], (B_SZ, L_SEQ, HIDDEN), jnp.float32), 'in_proj_w': jax.random.normal(ks[1], (2 * INTER, HIDDEN), jnp.float32) * s(HIDDEN), 'conv_w': jax.random.normal(ks[2], (INTER, 1, KCONV), jnp.float32) * s(KCONV), 'conv_b': jax.random.normal(ks[3], (INTER,), jnp.float32) * 0.01, 'x_proj_w': jax.random.normal(ks[4], (DT_RANK + 2 * STATE, INTER), jnp.float32) * s(INTER), 'dt_proj_w': jax.random.normal(ks[5], (INTER, DT_RANK), jnp.float32) * s(DT_RANK), 'dt_proj_b': jax.random.uniform(ks[6], (INTER,), jnp.float32, -4.0, -1.0), 'A_log': jnp.log(jnp.broadcast_to(jnp.arange(1, STATE + 1, dtype=jnp.float32)[None, :], (INTER, STATE))), 'D_param': jnp.ones((INTER,), jnp.float32), 'out_proj_w': jax.random.normal(ks[7], (HIDDEN, INTER), jnp.float32) * s(INTER)}
        return inp
    _L0_attn_b_in = _L0_attn_b_setup()

    def _L0_ffn_setup():
        import jax, jax.numpy as jnp
        import numpy as np
        HIDDEN = 512
        INTER = 1376
        LUT_SIZE = 16

        def _ghost_linear(x, idx, lut):
            w = lut[idx]
            return jnp.einsum('bsh,oh->bso', x, w)
        key = jax.random.key(seed)
        k_x, k_lut, k_g, k_u, k_d = jax.random.split(key, 5)
        x = jax.random.normal(k_x, (2, 1024, HIDDEN), dtype=jnp.float32)
        lut = jax.random.normal(k_lut, (LUT_SIZE,), dtype=jnp.float32) * 0.02
        gate_idx = jax.random.randint(k_g, (INTER, HIDDEN), 0, LUT_SIZE, dtype=jnp.int32)
        up_idx = jax.random.randint(k_u, (INTER, HIDDEN), 0, LUT_SIZE, dtype=jnp.int32)
        down_idx = jax.random.randint(k_d, (HIDDEN, INTER), 0, LUT_SIZE, dtype=jnp.int32)
        return {'x': x, 'lut': lut, 'gate_idx': gate_idx, 'up_idx': up_idx, 'down_idx': down_idx}
    _L0_ffn_in = _L0_ffn_setup()
    _d = {'L0_attn_a_x': _L0_attn_a_in['x'], 'L0_attn_a_W_rvk': _L0_attn_a_in['W_rvk'], 'L0_attn_a_W_out': _L0_attn_a_in['W_out'], 'L0_attn_a_time_decay': _L0_attn_a_in['time_decay'], 'L0_attn_a_time_first': _L0_attn_a_in['time_first'], 'L0_attn_b_in_proj_w': _L0_attn_b_in['in_proj_w'], 'L0_attn_b_conv_w': _L0_attn_b_in['conv_w'], 'L0_attn_b_conv_b': _L0_attn_b_in['conv_b'], 'L0_attn_b_x_proj_w': _L0_attn_b_in['x_proj_w'], 'L0_attn_b_dt_proj_w': _L0_attn_b_in['dt_proj_w'], 'L0_attn_b_dt_proj_b': _L0_attn_b_in['dt_proj_b'], 'L0_attn_b_A_log': _L0_attn_b_in['A_log'], 'L0_attn_b_D_param': _L0_attn_b_in['D_param'], 'L0_attn_b_out_proj_w': _L0_attn_b_in['out_proj_w'], 'L0_ffn_lut': _L0_ffn_in['lut'], 'L0_ffn_gate_idx': _L0_ffn_in['gate_idx'], 'L0_ffn_up_idx': _L0_ffn_in['up_idx'], 'L0_ffn_down_idx': _L0_ffn_in['down_idx']}
    _x0 = _d['L0_attn_a_x']
    _d['L0_attn_a_x'] = jax.random.normal(jax.random.fold_in(jax.random.key(seed), 1), (2, 2048, 512), dtype=_x0.dtype)
    del _x0
    return _d

def reference(L0_attn_a_x, L0_attn_a_W_rvk, L0_attn_a_W_out, L0_attn_a_time_decay, L0_attn_a_time_first, L0_attn_b_in_proj_w, L0_attn_b_conv_w, L0_attn_b_conv_b, L0_attn_b_x_proj_w, L0_attn_b_dt_proj_w, L0_attn_b_dt_proj_b, L0_attn_b_A_log, L0_attn_b_D_param, L0_attn_b_out_proj_w, L0_ffn_lut, L0_ffn_gate_idx, L0_ffn_up_idx, L0_ffn_down_idx):

    def _L0_attn_a_ref(x, W_rvk, W_out, time_decay, time_first):
        import jax, jax.numpy as jnp
        import numpy as np
        B, T, C = (8, 256, 512)

        def wkv(time_decay, time_first, k, v):
            w = -jnp.exp(time_decay)
            u = time_first
            b, t, c = k.shape
            k_t = jnp.transpose(k, (1, 0, 2))
            v_t = jnp.transpose(v, (1, 0, 2))

            def step(carry, kv):
                p, q, o = carry
                kt, vt = kv
                no = jnp.maximum(o, u + kt)
                A = jnp.exp(o - no)
                Bc = jnp.exp(u + kt - no)
                y = (A * p + Bc * vt) / (A * q + Bc)
                no2 = jnp.maximum(w + o, kt)
                A2 = jnp.exp(w + o - no2)
                B2 = jnp.exp(kt - no2)
                return ((A2 * p + B2 * vt, A2 * q + B2, no2), y)
            init = (jnp.zeros((b, c), k.dtype), jnp.zeros((b, c), k.dtype), jnp.full((b, c), -1e+38, k.dtype))
            _, y = jax.lax.scan(step, init, (k_t, v_t))
            return jnp.transpose(y, (1, 0, 2))
        rvk = jnp.einsum('btc,dc->btd', x, W_rvk)
        r, v, k = jnp.split(rvk, 3, axis=-1)
        y = jax.nn.sigmoid(r) * wkv(time_decay, time_first, k, v)
        return jnp.einsum('btc,dc->btd', y, W_out)

    def _L0_attn_b_ref(hidden_states, in_proj_w, conv_w, conv_b, x_proj_w, dt_proj_w, dt_proj_b, A_log, D_param, out_proj_w):
        import jax, jax.numpy as jnp
        import numpy as np
        HIDDEN = 512
        INTER = 1024
        STATE = 16
        KCONV = 4
        DT_RANK = 128
        B_SZ = 2
        L_SEQ = 512

        def _mamba_forward(hidden_states, in_proj_w, conv_w, conv_b, x_proj_w, dt_proj_w, dt_proj_b, A_log, D_param, out_proj_w):
            Bsz, L, _ = hidden_states.shape
            proj = jnp.einsum('blh,eh->ble', hidden_states, in_proj_w)
            x, gate = (proj[..., :INTER], proj[..., INTER:])
            xc = jnp.swapaxes(x, 1, 2)
            xc = jax.lax.conv_general_dilated(xc, conv_w, window_strides=(1,), padding=[(KCONV - 1, 0)], dimension_numbers=('NCH', 'OIH', 'NCH'), feature_group_count=INTER)
            xc = jax.nn.silu(xc + conv_b[None, :, None])
            u = jnp.swapaxes(xc, 1, 2)
            ssm_p = jnp.einsum('bld,rd->blr', u, x_proj_w)
            dt_lr = ssm_p[..., :DT_RANK]
            Bm = ssm_p[..., DT_RANK:DT_RANK + STATE]
            Cm = ssm_p[..., DT_RANK + STATE:]
            delta = jax.nn.softplus(jnp.einsum('blr,dr->bld', dt_lr, dt_proj_w) + dt_proj_b)
            A = -jnp.exp(A_log)

            def step(h, xs):
                d_t, B_t, C_t, u_t = xs
                dA = jnp.exp(d_t[..., None] * A)
                h = h * dA + (d_t * u_t)[..., None] * B_t[:, None, :]
                y_t = jnp.einsum('bdn,bn->bd', h, C_t)
                return (h, y_t)
            h0 = jnp.zeros((Bsz, INTER, STATE), delta.dtype)
            xs = (jnp.moveaxis(delta, 1, 0), jnp.moveaxis(Bm, 1, 0), jnp.moveaxis(Cm, 1, 0), jnp.moveaxis(u, 1, 0))
            _, ys = jax.lax.scan(step, h0, xs)
            y = jnp.moveaxis(ys, 0, 1) + u * D_param
            y = y * jax.nn.silu(gate)
            return jnp.einsum('bld,hd->blh', y, out_proj_w)
        return _mamba_forward(hidden_states, in_proj_w, conv_w, conv_b, x_proj_w, dt_proj_w, dt_proj_b, A_log, D_param, out_proj_w)

    def _L0_ffn_ref(x, lut, gate_idx, up_idx, down_idx):
        import jax, jax.numpy as jnp
        import numpy as np
        HIDDEN = 512
        INTER = 1376
        LUT_SIZE = 16

        def _ghost_linear(x, idx, lut):
            w = lut[idx]
            return jnp.einsum('bsh,oh->bso', x, w)
        gate = _ghost_linear(x, gate_idx, lut)
        up = _ghost_linear(x, up_idx, lut)
        h = jax.nn.silu(gate) * up
        return _ghost_linear(h, down_idx, lut)
    x = L0_attn_a_x
    x = x + _L0_attn_a_ref(_layernorm(x, axis=-1), L0_attn_a_W_rvk, L0_attn_a_W_out, L0_attn_a_time_decay, L0_attn_a_time_first)
    x = x + _L0_ffn_ref(_layernorm(x, axis=-1), L0_ffn_lut, L0_ffn_gate_idx, L0_ffn_up_idx, L0_ffn_down_idx)
    x = x + _L0_attn_b_ref(_layernorm(x, axis=-1), L0_attn_b_in_proj_w, L0_attn_b_conv_w, L0_attn_b_conv_b, L0_attn_b_x_proj_w, L0_attn_b_dt_proj_w, L0_attn_b_dt_proj_b, L0_attn_b_A_log, L0_attn_b_D_param, L0_attn_b_out_proj_w)
    x = x + _L0_ffn_ref(_layernorm(x, axis=-1), L0_ffn_lut, L0_ffn_gate_idx, L0_ffn_up_idx, L0_ffn_down_idx)
    return x

_drawn_inputs = setup_inputs


def setup_inputs(seed=0):
    import zlib

    import numpy as np

    out = dict(_drawn_inputs(seed))
    spreads = {'L0_attn_b_D_param': (1.0, 0.2)}
    factors = {'L0_attn_a_time_decay': 2.996, 'L0_attn_a_time_first': 4.102, 'L0_attn_b_conv_b': 8.0}
    for name, (base, spread) in spreads.items():
        noise = np.random.default_rng([zlib.crc32(name.encode()), seed]).standard_normal(out[name].shape)
        drawn = base * np.exp(spread * noise) if base else spread * noise
        out[name] = jnp.asarray(drawn.astype(out[name].dtype))
    for name, factor in factors.items():
        out[name] = (out[name] * factor).astype(out[name].dtype)
    return out
```

```python
from contextlib import ExitStack

import concourse.bass as bass
from concourse import mybir

ALU = mybir.AluOpType
ACT = mybir.ActivationFunctionType
F32 = mybir.dt.float32
I32 = mybir.dt.int32

P = 128
CH = 256
TT = CH // P
EPS = 1e-5
FLOOR = -1e38
DEC = 520

F2_SILU = (4, 7, 10, 13, 16, 18)
F2_RES = 29
F1_STAT = 20
F1_NORM = 22
F1_EVAC = 31
F1_SILU = (34, 37, 40, 43, 46, 48)


def hybrid_block_kernel(
    nc, x, w_rvk, w_out, decay, first, idx, lut, w_in, conv_w, conv_b, w_x, w_dt, b_dt, a_log, d_skip, w_o, inner, out
):
    N, H = x.shape
    KH = H // P
    NC = N // CH
    SEQ = NC // 2
    E = w_in.shape[1] // 2
    ME = E // P
    S = a_log.shape[2]
    R = w_dt.shape[0]
    KC = conv_w.shape[2]
    IN = inner
    MI = -(-IN // P)
    LAST = IN - (MI - 1) * P
    GU = KH * IN
    WF = 2 * GU + MI * H
    PIECES = WF // DEC
    NP = (MI + 1) // 2
    NE = S * ME // 2
    assert WF == idx.shape[1] and WF % DEC == 0 and PIECES == 2 * NC and R == P and KC == 4

    def least(n):
        return max(n, 0) if isinstance(n, int) else n

    x_t = x.rearrange("(c t p) d -> c p t d", t=TT, p=P)
    out_t = out.rearrange("(c t p) d -> c p t d", t=TT, p=P)
    x1_d = nc.dram_tensor("x1_scratch", (N, H), F32, kind="Internal").ap().rearrange("(c t p) d -> c p t d", t=TT, p=P)
    x2_d = nc.dram_tensor("x2_scratch", (N, H), F32, kind="Internal").ap().rearrange("(c t p) d -> c p t d", t=TT, p=P)
    bc_d = nc.dram_tensor("bc_scratch", (NC, 2, S, CH), F32, kind="Internal").ap()

    with ExitStack() as ctx:
        sem = lambda name: ctx.enter_context(nc.semaphore(name))

        def buf(stack, name, shape, dt=F32):
            return stack.enter_context(nc.sbuf_tensor(name, [P] + shape, dt))

        wffn = buf(ctx, "wffn", [WF])
        wg = wffn[:, 0:GU].rearrange("p (k n) -> p k n", k=KH)
        wu = wffn[:, GU:2 * GU].rearrange("p (k n) -> p k n", k=KH)
        wd = wffn[:, 2 * GU:WF].rearrange("p (k n) -> p k n", k=MI)
        ident = buf(ctx, "ident", [P])
        keep = buf(ctx, "keep", [NC + 1])
        floor = buf(ctx, "floor", [NC + 1])
        mhalf = buf(ctx, "mhalf", [TT])
        bnst = buf(ctx, "bnst", [TT, 6])
        mv = buf(ctx, "mv", [TT, 2])
        veps = buf(ctx, "veps", [TT])
        tick = buf(ctx, "tick", [1])
        rstd = buf(ctx, "rstd", [TT])

        const_ready = sem("const_ready")
        ident_zero = sem("ident_zero")
        par_loaded = sem("par_loaded")
        x_loaded = [sem(f"x_loaded{s}") for s in range(2)]
        xr_loaded = sem("xr_loaded")
        x1_stored = sem("x1_stored")
        idx_loaded = [sem(f"idx_loaded{h}") for h in range(2)]
        dec_ready = sem("dec_ready")
        dec_step = sem("dec_step")
        dec_stored = [sem(f"dec_stored{h}") for h in range(2)]
        a_stat, a_var, a_veps, a_rstd, a_xn = sem("a_stat"), sem("a_var"), sem("a_veps"), sem("a_rstd"), sem("a_xn")
        a_tr, a_xnT, a_rvk, a_evac = sem("a_tr"), sem("a_xnT"), sem("a_rvk"), sem("a_evac")
        a_carry, a_o, a_z, a_dd, a_kko = sem("a_carry"), sem("a_o"), sem("a_z"), sem("a_dd"), sem("a_kko")
        a_eo, a_ek, a_kv, a_relu, a_mix, a_pq = sem("a_eo"), sem("a_ek"), sem("a_kv"), sem("a_relu"), sem("a_mix"), sem("a_pq")
        a_bv, a_old, a_num, a_den, a_nsig = sem("a_bv"), sem("a_old"), sem("a_num"), sem("a_den"), sem("a_nsig")
        a_ln, a_r0, a_nt, a_rec, a_y = sem("a_ln"), sem("a_r0"), sem("a_nt"), sem("a_rec"), sem("a_y")
        a_out, a_resid = sem("a_out"), sem("a_resid")
        setup_step = sem("setup_step")

        with ExitStack() as pa:
            wr = buf(pa, "wr", [KH, 3 * H])
            wo1 = buf(pa, "wo1", [KH, H])
            dec = buf(pa, "dec", [KH])
            fst = buf(pa, "fst", [KH])
            nfst = buf(pa, "nfst", [KH])
            lutS = buf(pa, "lutS", [16])
            lutX = buf(pa, "lutX", [8], I32)
            X = [buf(pa, f"X{s}", [TT, H]) for s in range(2)]
            XR = buf(pa, "XR", [TT, H])
            xn = buf(pa, "xn", [TT, H])
            xnT = buf(pa, "xnT", [KH, CH])
            sg = [buf(pa, f"sg{s}", [KH, CH]) for s in range(2)]
            vv = [buf(pa, f"vv{s}", [KH, CH]) for s in range(2)]
            kk = [buf(pa, f"kk{s}", [KH, CH]) for s in range(2)]
            oX = buf(pa, "oX", [KH, CH + 1])
            pX = buf(pa, "pX", [KH, CH + 1])
            qX = buf(pa, "qX", [KH, CH + 1])
            EO = buf(pa, "EO", [KH, CH])
            EK = buf(pa, "EK", [KH, CH])
            Z = buf(pa, "Z", [KH, CH])
            M = buf(pa, "M", [KH, CH])
            MA = buf(pa, "MA", [KH, CH])
            MB = buf(pa, "MB", [KH, CH])
            yT = buf(pa, "yT", [KH, CH])
            ix = [buf(pa, f"ix{s}", [DEC], I32) for s in range(2)]
            bit = [buf(pa, f"bit{b}", [DEC], I32) for b in range(4)]
            nA = [buf(pa, f"nA{s}", [DEC], I32) for s in range(2)]
            nB, nC, nE = (buf(pa, f"n{c}", [DEC], I32) for c in "BCE")
            trP = pa.enter_context(nc.psum_tensor("trP", [P, KH, CH], F32))
            rvkP = [pa.enter_context(nc.psum_tensor(f"rvkP{s}", [P, KH, CH], F32)) for s in range(2)]
            outP = pa.enter_context(nc.psum_tensor("outP", [P, TT, H], F32))
            block = pa.enter_context(nc.Block())

            def steps_a(step, eng):
                step(-1, 1, True, False)
                step(0, 0, True, True)
                step(1, 1, True, True)
                with eng.Fori(2, NC - 3, 2) as c:
                    step(c, 0, True, True)
                    step(c + 1, 1, True, True)
                step(NC - 2, 0, True, True)
                step(NC - 1, 1, False, True)

            @block.sync
            def _(sp):
                sp.dma_start(X[0][:], x_t[0]).then_inc(x_loaded[0], 16)
                sp.dma_start(wr[:], w_rvk.rearrange("(k p) n -> p k n", p=P)).then_inc(par_loaded, 16)
                sp.dma_start(dec[:], decay).then_inc(par_loaded, 16)
                sp.dma_start(fst[:], first).then_inc(par_loaded, 16)
                sp.dma_start(lutS[:], lut.partition_broadcast(P)).then_inc(par_loaded, 16)
                sp.dma_start(wo1[:], w_out.rearrange("(k p) n -> p k n", p=P)).then_inc(par_loaded, 16)
                sp.dma_start(X[1][:], x_t[1]).then_inc(x_loaded[1], 16)
                for q in range(2):
                    sp.dma_start(ix[q][:], idx[:, q * DEC:(q + 1) * DEC]).then_inc(idx_loaded[q], 16)

                def step(c, s, more_x, more_idx):
                    if more_x:
                        sp.wait_ge(a_xn, TT * (c + 1))
                        sp.wait_ge(par_loaded, 80)
                        sp.dma_start(X[s][:], x_t[c + 2]).then_inc(x_loaded[s], 16)
                    sp.wait_ge(x1_stored, 16 * c)
                    sp.wait_ge(par_loaded, 80)
                    sp.dma_start(XR[:], x_t[c]).then_inc(xr_loaded, 16)
                    for h in range(2):
                        q = 2 * c + h
                        sp.wait_ge(dec_ready, q + 1)
                        sp.wait_ge(par_loaded, 80)
                        sp.dma_start(wffn[:, bass.ds(q * DEC, DEC)], nA[h][:].bitcast(F32)).then_inc(dec_stored[h], 16)
                        if more_idx:
                            sp.dma_start(ix[h][:], idx[:, bass.ds((q + 2) * DEC, DEC)]).then_inc(idx_loaded[h], 16)
                    sp.wait_ge(a_resid, c + 1)
                    sp.wait_ge(par_loaded, 80)
                    sp.dma_start(x1_d[c], XR[:]).then_inc(x1_stored, 16)

                step(0, 0, True, True)
                step(1, 1, True, True)
                with sp.Fori(2, NC - 3, 2) as c:
                    step(c, 0, True, True)
                    step(c + 1, 1, True, True)
                step(NC - 2, 0, False, True)
                step(NC - 1, 1, False, False)
                sp.wait_ge(x1_stored, 16 * NC)
                for h in range(2):
                    sp.wait_ge(dec_stored[h], 16 * NC)

            @block.gpsimd
            def _(pool):
                nc.gpsimd.memset(ident[:], 0.0).then_inc(ident_zero, 1)
                nc.gpsimd.memset(mhalf[:], -0.5).then_inc(const_ready, 1)
                pool.wait_ge(ident_zero, 1)
                nc.gpsimd.affine_select(out=ident[:], in_=ident[:], compare_op=ALU.not_equal, fill=1.0, base=0,
                                        pattern=[[-1, P]], channel_multiplier=1).then_inc(const_ready, 1)
                pool.wait_ge(const_ready, 2)

                def step(c, s, front, back):
                    if front:
                        pool.wait_ge(a_veps, c + 2)
                        nc.gpsimd.tensor_tensor(rstd[:], veps[:], mhalf[:], ALU.pow).then_inc(a_rstd, 1)
                    if back:
                        pool.wait_ge(a_o, KH * (c + 1))
                        pool.wait_ge(a_pq, 2 * KH * c)
                        nc.gpsimd.tensor_tensor(EO[:], oX[:, :, 0:CH], oX[:, :, 1:CH + 1], ALU.subtract).then_inc(a_dd, 1)
                        nc.gpsimd.tensor_tensor(EK[:], kk[s][:], oX[:, :, 1:CH + 1], ALU.subtract).then_inc(a_kko, 1)
                        pool.wait_ge(a_ek, c + 1)
                        pool.wait_ge(a_nt, c)
                        nc.gpsimd.tensor_tensor(M[:], EK[:], vv[s][:], ALU.mult).then_inc(a_kv, 1)
                        pool.wait_ge(a_mix, c + 1)
                        pool.wait_ge(a_kv, c + 1)
                        nc.gpsimd.tensor_tensor(vv[s][:], MB[:], vv[s][:], ALU.mult).then_inc(a_bv, 1)
                        pool.wait_ge(a_num, c + 1)
                        nc.gpsimd.tensor_tensor(Z[:], Z[:], sg[s][:], ALU.mult).then_inc(a_nsig, 1)

                steps_a(step, pool)

            @block.scalar
            def _(act):
                act.wait_ge(par_loaded, 80)
                nc.scalar.activation(dec[:], dec[:], ACT.Exp).then_inc(setup_step, 1)

                def step(c, s, front, back):
                    f, sf = c + 1, 1 - s
                    if front:
                        act.wait_ge(a_tr, f + 1)
                        act.wait_ge(a_rvk, 3 * f)
                        nc.scalar.activation(xnT[:], trP[:], ACT.Copy).then_inc(a_xnT, 1)
                    if back:
                        act.wait_ge(a_dd, c + 1)
                        act.wait_ge(setup_step, 4)
                        for m in range(KH):
                            nc.scalar.activation(EO[:, m, :], EO[:, m, :], ACT.Exp, bias=dec[:, m:m + 1]).then_inc(a_eo, 1)
                        act.wait_ge(a_kko, c + 1)
                        nc.scalar.activation(EK[:], EK[:], ACT.Exp).then_inc(a_ek, 1)
                    if front:
                        act.wait_ge(a_rvk, 3 * f + 1)
                        act.wait_ge(a_nsig, least(f - 1))
                        nc.scalar.activation(sg[sf][:], rvkP[sf][:], ACT.Sigmoid).then_inc(a_evac, 1)
                    if back:
                        act.wait_ge(a_z, c + 1)
                        act.wait_ge(a_y, c)
                        for m in range(KH):
                            nc.scalar.activation(MA[:, m, :], Z[:, m, :], ACT.Relu, bias=fst[:, m:m + 1]).then_inc(a_relu, 1)
                        for m in range(KH):
                            nc.scalar.activation(MB[:, m, :], Z[:, m, :], ACT.Relu, bias=nfst[:, m:m + 1], scale=-1.0).then_inc(a_relu, 1)
                        act.wait_ge(a_relu, 2 * KH * (c + 1))
                        nc.scalar.activation(MA[:], MA[:], ACT.Exp, scale=-1.0)
                        nc.scalar.activation(MB[:], MB[:], ACT.Exp, scale=-1.0).then_inc(a_mix, 1)
                    if front:
                        act.wait_ge(a_rvk, 3 * f + 2)
                        act.wait_ge(a_num, least(f - 1))
                        nc.scalar.activation(vv[sf][:], rvkP[1 - sf][:], ACT.Copy).then_inc(a_evac, 1)
                    if back:
                        act.wait_ge(a_den, c + 1)
                        nc.scalar.activation(MA[:], M[:], ACT.Ln).then_inc(a_ln, 1)
                        act.wait_ge(a_ln, c + 1)
                        nc.scalar.activation(MA[:], MA[:], ACT.Exp, scale=-1.0).then_inc(a_r0, 1)
                    if front:
                        act.wait_ge(a_rvk, 3 * f + 3)
                        act.wait_ge(a_z, least(f - 1))
                        act.wait_ge(a_kko, least(f - 1))
                        nc.scalar.activation(kk[sf][:], rvkP[sf][:], ACT.Copy).then_inc(a_evac, 1)

                steps_a(step, act)

            @block.tensor
            def _(pe):
                pe.wait_ge(const_ready, 2)
                pe.wait_ge(par_loaded, 80)

                def step(c, s, front, back):
                    f, sf = c + 1, 1 - s
                    if front:
                        pe.wait_ge(a_xn, TT * (f + 1))
                        pe.wait_ge(a_xnT, f)
                        for k in range(KH):
                            for t in range(TT):
                                last = nc.tensor.transpose(trP[:, k, t * P:(t + 1) * P], xn[:, t, k * P:(k + 1) * P], ident[:])
                        last.then_inc(a_tr, 1)
                        pe.wait_ge(a_xnT, f + 1)
                        for g in range(3):
                            pe.wait_ge(a_evac, least(3 * f + g - 1))
                            for m in range(KH):
                                for k in range(KH):
                                    last = nc.tensor.matmul(rvkP[(sf + g) % 2][:, m, :], wr[:, k, g * H + m * P:g * H + (m + 1) * P],
                                                            xnT[:, k, :], start=(k == 0), stop=(k == KH - 1))
                            last.then_inc(a_rvk, 1)
                    if back:
                        pe.wait_ge(a_y, c + 1)
                        pe.wait_ge(a_resid, c)
                        for t in range(TT):
                            for k in range(KH):
                                last = nc.tensor.matmul(outP[:, t, :], yT[:, k, t * P:(t + 1) * P], wo1[:, k, :],
                                                        start=(k == 0), stop=(k == KH - 1))
                        last.then_inc(a_out, 1)

                steps_a(step, pe)

            @block.vector
            def _(dve):
                V = nc.vector
                V.memset(keep[:], 1.0)
                V.memset(floor[:], 0.0)
                for t in (oX, pX, qX):
                    V.memset(t[:, :, CH:CH + 1], 0.0)
                V.memset(veps[:], 1.0).then_inc(setup_step, 1)
                dve.wait_ge(setup_step, 2)
                V.memset(keep[:, 0:NC:SEQ], 0.0)
                V.memset(floor[:, 0:NC:SEQ], FLOOR)
                V.tensor_scalar(dec[:], dec[:], -1.0, None, ALU.mult).then_inc(setup_step, 1)
                lutI = lutS[:].bitcast(I32).rearrange("p (a b) -> p a b", b=2)
                V.tensor_tensor(lutX[:], lutI[:, :, 0], lutI[:, :, 1], ALU.bitwise_xor)
                V.tensor_scalar(nfst[:], fst[:], -1.0, None, ALU.mult).then_inc(setup_step, 1)
                dve.wait_ge(setup_step, 4)

                def alone(semaphore, count):
                    dve.wait_ge(semaphore, count)
                    V.memset(tick[:], 0.0)

                def decode(c, h):
                    q, a = 2 * c + h, nA[h]

                    def leaf(dst, j, k=0):
                        if k:
                            dve.wait_ge(dec_step, 18 * q + k)
                        return V.tensor_scalar(dst[:], bit[0][:], lutX[:, j:j + 1], lutI[:, j, 0:1], ALU.bitwise_and, ALU.bitwise_xor)

                    def pick(dst, b, src, k=0):
                        if k:
                            alone(dec_step, 18 * q + k)
                        return V.copy_predicated(dst[:], bit[b][:], src[:])

                    dve.wait_ge(idx_loaded[h], 16 * (c + 1))
                    dve.wait_ge(dec_ready, q)
                    V.tensor_scalar(bit[0][:], ix[h][:], 31, 31, ALU.logical_shift_left, ALU.arith_shift_right).then_inc(dec_step, 1)
                    for b in range(1, 4):
                        V.tensor_scalar(bit[b][:], ix[h][:], 1 << b, None, ALU.bitwise_and).then_inc(dec_step, 1)
                    dve.wait_ge(dec_stored[h], 16 * c)
                    dve.wait_ge(dec_step, 18 * q + 1)
                    leaf(a, 0).then_inc(dec_step, 1)
                    leaf(nB, 1).then_inc(dec_step, 1)
                    leaf(nC, 2, 6).then_inc(dec_step, 1)
                    pick(a, 1, nB).then_inc(dec_step, 1)
                    leaf(nB, 3, 8).then_inc(dec_step, 1)
                    leaf(nE, 4, 9).then_inc(dec_step, 1)
                    pick(nC, 1, nB).then_inc(dec_step, 1)
                    leaf(nB, 5, 11).then_inc(dec_step, 1)
                    pick(a, 2, nC).then_inc(dec_step, 1)
                    leaf(nC, 6, 13).then_inc(dec_step, 1)
                    pick(nE, 1, nB).then_inc(dec_step, 1)
                    leaf(nB, 7, 15).then_inc(dec_step, 1)
                    pick(nC, 1, nB, 16).then_inc(dec_step, 1)
                    pick(nE, 2, nC, 17).then_inc(dec_step, 1)
                    pick(a, 3, nE, 18).then_inc(dec_ready, 1)

                def resid(c):
                    dve.wait_ge(a_out, c + 1)
                    dve.wait_ge(xr_loaded, 16 * (c + 1))
                    V.tensor_tensor(XR[:], outP[:], XR[:], ALU.add).then_inc(a_resid, 1)

                def step(c, s, front, back):
                    f, sf = c + 1, 1 - s
                    if front:
                        dve.wait_ge(x_loaded[sf], 8 * (f - sf) + 16)
                        dve.wait_ge(a_var, TT * f)
                        for t in range(TT):
                            V.bn_stats(bnst[:, t, :], X[sf][:, t, :]).then_inc(a_stat, 1)
                        dve.wait_ge(a_xn, TT * f)
                        alone(a_stat, TT * (f + 1))
                        for t in range(TT):
                            V.bn_aggr(mv[:, t, :], bnst[:, t, :]).then_inc(a_var, 1)
                        dve.wait_ge(a_var, TT * (f + 1))
                        dve.wait_ge(a_rstd, f)
                        V.tensor_scalar(veps[:], mv[:, :, 1], EPS, None, ALU.add).then_inc(a_veps, 1)
                    if back:
                        dve.wait_ge(a_dd, c)
                        dve.wait_ge(a_old, 2 * c)
                        V.tensor_scalar(oX[:, :, 0:1], oX[:, :, CH:CH + 1], keep[:, bass.ds(c, 1)], floor[:, bass.ds(c, 1)],
                                        ALU.mult, ALU.add).then_inc(a_carry, 1)
                        V.tensor_scalar(pX[:, :, 0:1], pX[:, :, CH:CH + 1], keep[:, bass.ds(c, 1)], None, ALU.mult).then_inc(a_carry, 1)
                        V.tensor_scalar(qX[:, :, 0:1], qX[:, :, CH:CH + 1], keep[:, bass.ds(c, 1)], None, ALU.mult).then_inc(a_carry, 1)
                        dve.wait_ge(a_evac, 3 * (c + 1))
                        dve.wait_ge(a_carry, 3 * (c + 1))
                        for m in range(KH):
                            V.tensor_tensor_scan(oX[:, m, 1:CH + 1], dec[:, m:m + 1].to_broadcast([P, CH]), kk[s][:, m, :],
                                                 oX[:, m, 0:1], ALU.add, ALU.max).then_inc(a_o, 1)
                    if front:
                        dve.wait_ge(a_rstd, f + 1)
                        dve.wait_ge(a_tr, f)
                        for t in range(TT):
                            V.tensor_scalar(xn[:, t, :], X[sf][:, t, :], mv[:, t, 0:1], rstd[:, t:t + 1],
                                            ALU.subtract, ALU.mult).then_inc(a_xn, 1)
                    if back:
                        dve.wait_ge(a_o, KH * (c + 1))
                        V.tensor_tensor(Z[:], kk[s][:], oX[:, :, 0:CH], ALU.subtract).then_inc(a_z, 1)
                        if not (isinstance(c, int) and c == 0):
                            resid(c - 1)
                        decode(c, 0)
                        dve.wait_ge(a_eo, KH * (c + 1))
                        dve.wait_ge(a_kv, c + 1)
                        for m in range(KH):
                            V.tensor_tensor_scan(pX[:, m, 1:CH + 1], EO[:, m, :], M[:, m, :], pX[:, m, 0:1], ALU.mult, ALU.add).then_inc(a_pq, 1)
                            V.tensor_tensor_scan(qX[:, m, 1:CH + 1], EO[:, m, :], EK[:, m, :], qX[:, m, 0:1], ALU.mult, ALU.add).then_inc(a_pq, 1)
                        dve.wait_ge(a_mix, c + 1)
                        dve.wait_ge(a_pq, 2 * KH * (c + 1))
                        V.tensor_tensor(Z[:], MA[:], pX[:, :, 0:CH], ALU.mult).then_inc(a_old, 1)
                        V.tensor_tensor(M[:], MA[:], qX[:, :, 0:CH], ALU.mult).then_inc(a_old, 1)
                        dve.wait_ge(a_old, 2 * (c + 1))
                        V.tensor_tensor(M[:], M[:], MB[:], ALU.add).then_inc(a_den, 1)
                        dve.wait_ge(a_bv, c + 1)
                        V.tensor_tensor(Z[:], Z[:], vv[s][:], ALU.add).then_inc(a_num, 1)
                        decode(c, 1)
                        dve.wait_ge(a_r0, c + 1)
                        V.tensor_tensor(MB[:], M[:], MA[:], ALU.mult).then_inc(a_nt, 1)
                        dve.wait_ge(a_nt, c + 1)
                        V.scalar_tensor_tensor(MB[:], MB[:], 2.0, MA[:], ALU.subtract, ALU.mult, reverse0=True).then_inc(a_rec, 1)
                        dve.wait_ge(a_rec, c + 1)
                        dve.wait_ge(a_nsig, c + 1)
                        dve.wait_ge(a_out, c)
                        V.tensor_tensor(yT[:], Z[:], MB[:], ALU.mult).then_inc(a_y, 1)

                steps_a(step, dve)
                resid(NC - 1)

        win = buf(ctx, "win", [KH, 2 * E])
        wx = buf(ctx, "wx", [ME, R + 2 * S])
        wdt = buf(ctx, "wdt", [E])
        wo = buf(ctx, "wo", [ME, H])
        cw = buf(ctx, "cw", [ME, KC])
        cb = buf(ctx, "cb", [ME])
        bdt = buf(ctx, "bdt", [ME])
        dsk = buf(ctx, "dsk", [ME])
        A = buf(ctx, "A", [ME, S])
        XM = buf(ctx, "XM", [TT, H])
        X3 = buf(ctx, "X3", [TT, H])
        nrm = buf(ctx, "nrm", [TT, H])
        nT = buf(ctx, "nT", [KH, CH])
        hT = buf(ctx, "hT", [MI, CH])
        U = buf(ctx, "U", [ME, CH])
        delta = buf(ctx, "delta", [ME, CH])
        yacc = buf(ctx, "yacc", [ME, CH])
        sgm = buf(ctx, "sgm", [ME, CH])
        bcS = buf(ctx, "bcS", [CH])
        dtl = buf(ctx, "dtl", [CH])
        xext = [buf(ctx, f"xext{s}", [2, CH + KC - 1]) for s in range(2)]
        cc = buf(ctx, "cc", [ME, KC - 1])
        hc = buf(ctx, "hc", [S, ME])
        BC = [buf(ctx, f"BC{s}", [2, CH]) for s in range(3)]
        dBu = [buf(ctx, f"dBu{s}", [2, CH]) for s in range(4)]
        prod = [buf(ctx, f"prod{s}", [2, CH]) for s in range(2)]
        W = [ctx.enter_context(nc.psum_tensor(f"W{s}", [P, 4, CH], F32)) for s in range(2)]
        D = ctx.enter_context(nc.psum_tensor("D", [P, ME, CH], F32))

        wts_loaded, small_loaded = sem("wts_loaded"), sem("small_loaded")
        b_setup = sem("b_setup")
        xm_loaded, x2_stored, x3_loaded, out_stored = sem("xm_loaded"), sem("x2_stored"), sem("x3_loaded"), sem("out_stored")
        bc_stored = sem("bc_stored")
        bc_loaded = [sem(f"bc_loaded{s}") for s in range(3)]
        n_stat, n_var, n_veps, n_rstd, n_done = sem("n_stat"), sem("n_var"), sem("n_veps"), sem("n_rstd"), sem("n_done")
        n_tr, n_T = sem("n_tr"), sem("n_T")
        f_gu, f_silu, f_h, f_out, f_res = sem("f_gu"), sem("f_silu"), sem("f_h"), sem("f_out"), sem("f_res")
        m_x, m_ext, m_tap, m_in, m_conv, m_cc = sem("m_x"), sem("m_ext"), sem("m_tap"), sem("m_in"), sem("m_conv"), sem("m_cc")
        m_u, m_skip, m_g, m_sg, m_bc, m_bcS = sem("m_u"), sem("m_skip"), sem("m_g"), sem("m_sg"), sem("m_bc"), sem("m_bcS")
        m_dt, m_dtl, m_dp, m_abs, m_relu = sem("m_dt"), sem("m_dtl"), sem("m_dp"), sem("m_abs"), sem("m_relu")
        m_exp, m_ln, m_delta, m_du = sem("m_exp"), sem("m_ln"), sem("m_delta"), sem("m_du")
        s_dA, s_dBu, s_scan, s_hc, s_prod, s_acc = sem("s_dA"), sem("s_dBu"), sem("s_scan"), sem("s_hc"), sem("s_prod"), sem("s_acc")
        m_y, m_out, m_res = sem("m_y"), sem("m_out"), sem("m_res")

        def first_step(i):
            return isinstance(i, int) and i == 0

        def norm_f1(i):
            return 0 if first_step(i) else 3 * i - 1

        def norm_m(i):
            return 1 if first_step(i) else 3 * i

        def norm_f2(i):
            return 3 * NC - 1 if isinstance(i, int) and i == NC - 1 else 3 * i + 4

        def ffn_1(i):
            return 0 if first_step(i) else 2 * i - 1

        def ffn_2(i):
            return 2 * NC - 1 if isinstance(i, int) and i == NC - 1 else 2 * i + 2

        def steps_b(step, eng):
            step(0, False, True)
            with eng.Fori(1, NC - 1) as i:
                step(i, True, True)
            step(NC - 1, True, False)

        def rows(p):
            return [(m, LAST if m == MI - 1 else P) for m in (2 * p, 2 * p + 1) if m < MI]

        with nc.Block() as block:
            @block.sync
            def _(sp):
                sp.dma_start(XM[:], x1_d[0]).then_inc(xm_loaded, 16)
                sp.dma_start(win[:], w_in.rearrange("(k p) n -> p k n", p=P)).then_inc(wts_loaded, 16)
                sp.dma_start(wx[:], w_x.rearrange("(k p) n -> p k n", p=P)).then_inc(wts_loaded, 16)
                sp.dma_start(wdt[:], w_dt).then_inc(wts_loaded, 16)
                sp.dma_start(wo[:], w_o.rearrange("(k p) n -> p k n", p=P)).then_inc(wts_loaded, 16)
                for t, d in ((cw, conv_w), (cb, conv_b), (bdt, b_dt), (dsk, d_skip), (A, a_log)):
                    sp.dma_start(t[:], d).then_inc(small_loaded, 16)

                def step(i, back, ahead):
                    sp.wait_ge(f_res, ffn_1(i) + 1)
                    sp.wait_ge(small_loaded, 80)
                    sp.dma_start(x2_d[i], XM[:]).then_inc(x2_stored, 16)
                    sp.wait_ge(x2_stored, 16 * (i + 1))
                    if ahead:
                        sp.wait_ge(n_done, TT * (norm_m(i) + 1))
                        sp.wait_ge(small_loaded, 80)
                        sp.dma_start(XM[:], x1_d[i + 1]).then_inc(xm_loaded, 16)
                    sp.wait_ge(m_bcS, i + 1)
                    sp.wait_ge(small_loaded, 80)
                    sp.dma_start(bc_d[i].rearrange("a n t -> (a n) t"), bcS[0:2 * S, :]).then_inc(bc_stored, 16)
                    sp.wait_ge(bc_stored, 16 * (i + 1))
                    sp.wait_ge(small_loaded, 80)
                    for n in range(S):
                        if n >= 3:
                            sp.wait_ge(s_prod, NE * i + 4 * (n - 2))
                            sp.wait_ge(small_loaded, 80)
                        sp.dma_start(BC[n % 3][:], bc_d[i][:, n, :].partition_broadcast(P)).then_inc(bc_loaded[n % 3], 16)
                        if n == 11:
                            if back:
                                sp.wait_ge(f_res, ffn_2(i - 1) + 1)
                                sp.wait_ge(small_loaded, 80)
                                sp.dma_start(out_t[i - 1], X3[:]).then_inc(out_stored, 16)
                        if n == 13:
                            sp.wait_ge(out_stored, 16 * i)
                            sp.wait_ge(small_loaded, 80)
                            sp.dma_start(X3[:], x2_d[i]).then_inc(x3_loaded, 16)

                steps_b(step, sp)
                sp.wait_ge(f_res, ffn_2(NC - 1) + 1)
                sp.dma_start(out_t[NC - 1], X3[:]).then_inc(out_stored, 16)
                sp.wait_ge(out_stored, 16 * NC)

            @block.gpsimd
            def _(pool):
                def root(L):
                    pool.wait_ge(n_veps, L + 1)
                    pool.wait_ge(n_done, TT * L)
                    nc.gpsimd.tensor_tensor(rstd[:], veps[:], mhalf[:], ALU.pow).then_inc(n_rstd, 1)

                def step(i, back, ahead):
                    root(norm_m(i))
                    if back:
                        root(norm_f2(i - 1))

                    def outer(e):
                        n, j = divmod(e, 4)
                        slot = n % 3
                        if j == 0:
                            pool.wait_ge(bc_loaded[slot], 16 * ((6 if slot == 0 else 5) * i + n // 3 + 1))
                        if e == 0:
                            pool.wait_ge(m_du, i + 1)
                        else:
                            pool.wait_ge(s_scan, 2 * NE * i + 2 * max(e - 3, 0))
                        nc.gpsimd.tensor_tensor(dBu[e % 4][:], U[:, 2 * j:2 * j + 2, :], BC[slot][:, 0:1, :].to_broadcast([P, 2, CH]),
                                                ALU.mult).then_inc(s_dBu, 1)

                    def add(e):
                        j = e % 4
                        pool.wait_ge(s_prod, NE * i + e + 1)
                        if e == 0:
                            pool.wait_ge(m_skip, ME * (i + 1))
                        if e >= 4:
                            pool.wait_ge(s_acc, NE * i + e - 3)
                        y = yacc[:, 2 * j:2 * j + 2, :]
                        nc.gpsimd.tensor_tensor(y, y, prod[e % 2][:], ALU.add).then_inc(s_acc, 1)

                    for e in range(4):
                        outer(e)
                    for e in range(NE):
                        if e + 4 < NE:
                            outer(e + 4)
                        add(e)
                        if ahead and e == F1_STAT + 1:
                            root(norm_f1(i + 1))

                root(0)
                steps_b(step, pool)
                root(norm_f2(NC - 1))

            @block.scalar
            def _(act):
                N_ = nc.scalar

                def evac(L):
                    act.wait_ge(n_tr, L + 1)
                    N_.activation(nT[:], W[0][:], ACT.Copy).then_inc(n_T, 1)

                def silu(F, L, p):
                    act.wait_ge(f_gu, NP * F + p + 1)
                    if p < 2:
                        act.wait_ge(n_tr, L + 1)
                    else:
                        act.wait_ge(f_h, NP * F + p - 1)
                    r = rows(p)
                    w = len(r) * CH
                    N_.activation(nrm[0:r[0][1], p % 2, 0:w], W[1 - p % 2][0:r[0][1], 0:len(r), :].rearrange("p a t -> p (a t)"),
                                  ACT.Silu).then_inc(f_silu, 1)

                def step(i, back, ahead):
                    evac(norm_m(i))
                    for q in range(ME // 2):
                        act.wait_ge(m_x, 2 * i + q // 2 + 1)
                        act.wait_ge(m_cc, 4 * i + max(q - 1, 0))
                        act.wait_ge(m_conv, 24 * i + 6 * max(q - 1, 0))
                        src = W[1 - q // 2]
                        a = 2 * (q % 2)
                        N_.activation(xext[q % 2][:, :, KC - 1:], src[:, a:a + 2, :], ACT.Copy).then_inc(m_ext, 1)
                        act.wait_ge(s_dBu, NE * i)
                        for h in range(2):
                            m = 2 * q + h
                            N_.activation(U[:, m, :], src[:, a + h, :], ACT.Identity, bias=cb[:, m:m + 1],
                                          scale=cw[:, m, KC - 1:KC]).then_inc(m_tap, 1)
                    for q in range(ME // 2):
                        act.wait_ge(m_conv, 24 * i + 6 * (q + 1))
                        N_.activation(U[:, 2 * q:2 * q + 2, :], U[:, 2 * q:2 * q + 2, :], ACT.Silu).then_inc(m_u, 1)
                    for h in range(2):
                        act.wait_ge(m_g, 2 * i + h + 1)
                        act.wait_ge(m_y, 2 * i)
                        N_.activation(sgm[:, 4 * h:4 * h + 4, :], W[h][:], ACT.Silu).then_inc(m_sg, 1)
                    act.wait_ge(m_u, 4 * (i + 1))
                    act.wait_ge(m_out, i)
                    for m in range(ME):
                        N_.activation(yacc[:, m, :], U[:, m, :], ACT.Identity, scale=dsk[:, m:m + 1]).then_inc(m_skip, 1)
                    act.wait_ge(m_bc, i + 1)
                    act.wait_ge(bc_stored, 16 * i)
                    N_.activation(bcS[0:2 * S, :], W[0][0:2 * S, 0, :], ACT.Copy).then_inc(m_bcS, 1)
                    act.wait_ge(m_dt, i + 1)
                    N_.activation(dtl[:], W[1][:, 0, :], ACT.Copy).then_inc(m_dtl, 1)
                    act.wait_ge(s_prod, NE * i)
                    act.wait_ge(s_dA, 2 * NE * i)
                    for h in range(2):
                        act.wait_ge(m_dp, 2 * i + h + 1)
                        for m in range(4 * h, 4 * h + 4):
                            N_.activation(D[:, m, :], W[h][:, m % 4, :], ACT.Abs, bias=bdt[:, m:m + 1]).then_inc(m_abs, 1)
                        for m in range(4 * h, 4 * h + 4):
                            N_.activation(delta[:, m, :], W[h][:, m % 4, :], ACT.Relu, bias=bdt[:, m:m + 1]).then_inc(m_relu, 1)
                    act.wait_ge(m_abs, ME * (i + 1))
                    N_.activation(D[:], D[:], ACT.Exp, scale=-1.0).then_inc(m_exp, 1)
                    act.wait_ge(m_exp, i + 1)
                    N_.activation(D[:], D[:], ACT.Ln, bias=1.0).then_inc(m_ln, 1)
                    act.wait_ge(m_delta, i + 1)
                    if back:
                        evac(norm_f2(i - 1))
                    for e in range(NE):
                        n, j = divmod(e, 4)
                        if e >= 4:
                            act.wait_ge(s_prod, NE * i + e - 3)
                        for m in (2 * j, 2 * j + 1):
                            N_.activation(D[:, m, :], delta[:, m, :], ACT.Exp, scale=A[:, m, n:n + 1]).then_inc(s_dA, 1)
                        for p in range(NP):
                            if back and e == F2_SILU[p]:
                                silu(ffn_2(i - 1), norm_f2(i - 1), p)
                            if ahead and e == F1_SILU[p]:
                                silu(ffn_1(i + 1), norm_f1(i + 1), p)
                        if ahead and e == F1_EVAC:
                            evac(norm_f1(i + 1))

                act.wait_ge(small_loaded, 80)
                N_.activation(A[:], A[:], ACT.Exp).then_inc(b_setup, 1)
                evac(0)
                for p in range(NP):
                    silu(0, 0, p)
                act.wait_ge(b_setup, 3)
                steps_b(step, act)
                evac(norm_f2(NC - 1))
                for p in range(NP):
                    silu(ffn_2(NC - 1), norm_f2(NC - 1), p)

            @block.tensor
            def _(pe):
                T_ = nc.tensor

                def chain(dst, terms):
                    for n, (lhsT, rhs) in enumerate(terms):
                        last = T_.matmul(dst, lhsT, rhs, start=(n == 0), stop=(n == len(terms) - 1))
                    return last

                def turn(L):
                    pe.wait_ge(n_done, TT * (L + 1))
                    for k in range(KH):
                        for t in range(TT):
                            last = T_.transpose(W[0][:, k, t * P:(t + 1) * P], nrm[:, t, k * P:(k + 1) * P], ident[:])
                    last.then_inc(n_tr, 1)

                def ffn(F, L):
                    for p in range(NP):
                        Wp = W[1 - p % 2]
                        if p < 2:
                            pe.wait_ge(n_T, L + 1)
                        else:
                            pe.wait_ge(f_h, NP * F + p - 1)
                        for half, wt in ((0, wg), (2, wu)):
                            for m, r in rows(p):
                                last = chain(Wp[0:r, half + m % 2, :], [(wt[:, k, m * P:m * P + r], nT[:, k, :]) for k in range(KH)])
                        last.then_inc(f_gu, 1)
                    pe.wait_ge(f_h, NP * F + NP)
                    for t in range(TT):
                        last = chain(W[1][:].rearrange("p (t a) n -> p t (a n)", t=TT)[:, t, :],
                                     [(hT[0:(LAST if k == MI - 1 else P), k, t * P:(t + 1) * P],
                                       wd[0:(LAST if k == MI - 1 else P), k, :]) for k in range(MI)])
                    last.then_inc(f_out, 1)

                def project(i):
                    pe.wait_ge(m_y, 2 * (i + 1))
                    for t in range(TT):
                        last = chain(W[1][:].rearrange("p (t a) n -> p t (a n)", t=TT)[:, t, :],
                                     [(yacc[:, k, t * P:(t + 1) * P], wo[:, k, :]) for k in range(ME)])
                    last.then_inc(m_out, 1)

                def step(i, back, ahead):
                    pe.wait_ge(f_h, NP * (ffn_1(i) + 1))
                    turn(norm_m(i))
                    pe.wait_ge(f_res, ffn_1(i) + 1)
                    pe.wait_ge(n_T, norm_m(i) + 1)
                    for h in range(2):
                        for m in range(4 * h, 4 * h + 4):
                            last = chain(W[1 - h][:, m % 4, :], [(win[:, k, m * P:(m + 1) * P], nT[:, k, :]) for k in range(KH)])
                        last.then_inc(m_x, 1)
                    if back:
                        pe.wait_ge(m_tap, ME * i + 4)
                        project(i - 1)
                    for h in range(2):
                        if h == 0:
                            pe.wait_ge(m_tap, ME * (i + 1))
                        else:
                            pe.wait_ge(m_res, i)
                        for m in range(4 * h, 4 * h + 4):
                            last = chain(W[h][:, m % 4, :], [(win[:, k, E + m * P:E + (m + 1) * P], nT[:, k, :]) for k in range(KH)])
                        last.then_inc(m_g, 1)
                    pe.wait_ge(m_u, 4 * (i + 1))
                    pe.wait_ge(m_sg, 2 * i + 1)
                    chain(W[0][0:2 * S, 0, :], [(wx[:, k, R:R + 2 * S], U[:, k, :]) for k in range(ME)]).then_inc(m_bc, 1)
                    pe.wait_ge(m_sg, 2 * i + 2)
                    chain(W[1][:, 0, :], [(wx[:, k, 0:R], U[:, k, :]) for k in range(ME)]).then_inc(m_dt, 1)
                    pe.wait_ge(m_bcS, i + 1)
                    pe.wait_ge(m_dtl, i + 1)
                    for h in range(2):
                        for m in range(4 * h, 4 * h + 4):
                            last = chain(W[h][:, m % 4, :], [(wdt[:, m * P:(m + 1) * P], dtl[:])])
                        last.then_inc(m_dp, 1)
                    pe.wait_ge(m_relu, ME * i + 4)
                    if back:
                        turn(norm_f2(i - 1))
                        pe.wait_ge(m_relu, ME * (i + 1))
                        ffn(ffn_2(i - 1), norm_f2(i - 1))
                        pe.wait_ge(f_h, NP * (ffn_2(i - 1) + 1))
                    if ahead:
                        turn(norm_f1(i + 1))
                        pe.wait_ge(m_relu, ME * (i + 1))
                        if back:
                            pe.wait_ge(f_res, ffn_2(i - 1) + 1)
                        ffn(ffn_1(i + 1), norm_f1(i + 1))

                turn(0)
                ffn(0, 0)
                pe.wait_ge(wts_loaded, 64)
                steps_b(step, pe)
                pe.wait_ge(f_res, ffn_2(NC - 2) + 1)
                project(NC - 1)
                turn(norm_f2(NC - 1))
                pe.wait_ge(m_res, NC)
                ffn(ffn_2(NC - 1), norm_f2(NC - 1))

            @block.vector
            def _(dve):
                V = nc.vector

                def alone(semaphore, count):
                    dve.wait_ge(semaphore, count)
                    V.memset(tick[:], 0.0)

                def stats(L, rows_):
                    dve.wait_ge(n_done, TT * L)
                    for t in range(TT):
                        V.bn_stats(bnst[:, t, :], rows_[:, t, :]).then_inc(n_stat, 1)
                    alone(n_stat, TT * (L + 1))
                    for t in range(TT):
                        V.bn_aggr(mv[:, t, :], bnst[:, t, :]).then_inc(n_var, 1)
                    dve.wait_ge(n_var, TT * (L + 1))
                    V.tensor_scalar(veps[:], mv[:, :, 1], EPS, None, ALU.add).then_inc(n_veps, 1)

                def norm(L, rows_):
                    dve.wait_ge(n_rstd, L + 1)
                    for t in range(TT):
                        V.tensor_scalar(nrm[:, t, :], rows_[:, t, :], mv[:, t, 0:1], rstd[:, t:t + 1],
                                        ALU.subtract, ALU.mult).then_inc(n_done, 1)

                def gated(F, p):
                    dve.wait_ge(f_silu, NP * F + p + 1)
                    if p == 0:
                        dve.wait_ge(f_out, F)
                    r = rows(p)
                    n, w = r[0][1], len(r)
                    V.tensor_tensor(hT[0:n, 2 * p:2 * p + w, :], nrm[0:n, p % 2, 0:w * CH].rearrange("p (a t) -> p a t", a=w),
                                    W[1 - p % 2][0:n, 2:2 + w, :], ALU.mult).then_inc(f_h, 1)

                def resid(ready, count, rows_, done):
                    dve.wait_ge(ready, count)
                    V.tensor_tensor(rows_[:].rearrange("p t d -> p (t d)"), W[1][:].rearrange("p a n -> p (a n)"),
                                    rows_[:].rearrange("p t d -> p (t d)"), ALU.add).then_inc(done, 1)

                def gate_y(i):
                    dve.wait_ge(s_acc, NE * (i + 1))
                    for h in range(2):
                        y = yacc[:, 4 * h:4 * h + 4, :]
                        V.tensor_tensor(y, y, sgm[:, 4 * h:4 * h + 4, :], ALU.mult).then_inc(m_y, 1)

                def out_resid(i):
                    dve.wait_ge(x3_loaded, 16 * (i + 1))
                    resid(m_out, i + 1, X3, m_res)

                def conv(i, q):
                    x_ = xext[q % 2]
                    cq = cc[:, 2 * q:2 * q + 2, :]
                    dve.wait_ge(m_conv, 24 * i + 6 * max(q - 1, 0))
                    dve.wait_ge(m_cc, 4 * i + max(q - 1, 0))
                    V.tensor_copy(x_[:, :, 0:KC - 1], cq).then_inc(m_in, 1)
                    dve.wait_ge(m_tap, ME * i + 2 * q + 2)
                    dve.wait_ge(m_in, 4 * i + q + 1)
                    for k in range(KC - 1):
                        for h in range(2):
                            m = 2 * q + h
                            if k:
                                dve.wait_ge(m_conv, 24 * i + 6 * q + 2 * (k - 1) + h + 1)
                            V.scalar_tensor_tensor(U[:, m, :], x_[:, h, k:k + CH], cw[:, m, k:k + 1], U[:, m, :],
                                                   ALU.mult, ALU.add).then_inc(m_conv, 1)
                    V.tensor_scalar(cq, x_[:, :, CH:CH + KC - 1], keep[:, bass.ds(i + 1, 1)], None, ALU.mult).then_inc(m_cc, 1)

                def step(i, back, ahead):
                    resid(f_out, ffn_1(i) + 1, XM, f_res)
                    dve.wait_ge(f_res, ffn_1(i) + 1)
                    stats(norm_m(i), XM)
                    if back:
                        gate_y(i - 1)
                    dve.wait_ge(f_h, NP * (ffn_1(i) + 1))
                    norm(norm_m(i), XM)
                    conv(i, 0)
                    conv(i, 1)
                    if back:
                        out_resid(i - 1)
                        dve.wait_ge(m_res, i)
                        stats(norm_f2(i - 1), X3)
                    conv(i, 2)
                    conv(i, 3)
                    if back:
                        dve.wait_ge(n_tr, norm_m(i) + 1)
                        norm(norm_f2(i - 1), X3)
                    dve.wait_ge(m_ln, i + 1)
                    V.tensor_tensor(delta[:], delta[:], D[:], ALU.add).then_inc(m_delta, 1)
                    dve.wait_ge(m_skip, ME * (i + 1))
                    dve.wait_ge(m_dt, i + 1)
                    dve.wait_ge(m_delta, i + 1)
                    V.tensor_tensor(U[:], U[:], delta[:], ALU.mult).then_inc(m_du, 1)
                    for e in range(NE + 1):
                        if e < NE:
                            n, j = divmod(e, 4)
                            for m in (2 * j, 2 * j + 1):
                                dve.wait_ge(s_dA, 2 * NE * i + 2 * e + 2)
                                dve.wait_ge(s_dBu, NE * i + e + 1)
                                dve.wait_ge(s_hc, NE * i)
                                V.tensor_tensor_scan(D[:, m, :], D[:, m, :], dBu[e % 4][:, m % 2, :], hc[:, n, m:m + 1],
                                                     ALU.mult, ALU.add).then_inc(s_scan, 1)
                        if e:
                            n, j = divmod(e - 1, 4)
                            dve.wait_ge(s_scan, 2 * NE * i + 2 * e)
                            V.tensor_scalar(hc[:, n, 2 * j:2 * j + 2], D[:, 2 * j:2 * j + 2, CH - 1], keep[:, bass.ds(i + 1, 1)], None,
                                            ALU.mult).then_inc(s_hc, 1)
                            dve.wait_ge(s_acc, NE * i + max(e - 2, 0))
                            dve.wait_ge(bc_loaded[n % 3], 16 * ((6 if n % 3 == 0 else 5) * i + n // 3 + 1))
                            V.tensor_tensor(prod[(e - 1) % 2][:], D[:, 2 * j:2 * j + 2, :], BC[n % 3][:, 1:2, :].to_broadcast([P, 2, CH]),
                                            ALU.mult).then_inc(s_prod, 1)
                        for p in range(NP):
                            if back and e == F2_SILU[p] + 1:
                                gated(ffn_2(i - 1), p)
                            if ahead and e == F1_SILU[p] + 1:
                                gated(ffn_1(i + 1), p)
                        if back and e == F2_RES:
                            resid(f_out, ffn_2(i - 1) + 1, X3, f_res)
                        if ahead and e == F1_STAT:
                            dve.wait_ge(xm_loaded, 16 * (i + 2))
                            stats(norm_f1(i + 1), XM)
                        if ahead and e == F1_NORM:
                            if back:
                                dve.wait_ge(f_h, NP * (ffn_2(i - 1) + 1))
                            norm(norm_f1(i + 1), XM)

                V.memset(hc[:], 0.0)
                V.memset(cc[:], 0.0).then_inc(b_setup, 1)
                dve.wait_ge(b_setup, 2)
                V.tensor_scalar(A[:], A[:], -1.0, None, ALU.mult).then_inc(b_setup, 1)
                dve.wait_ge(xm_loaded, 16)
                stats(0, XM)
                norm(0, XM)
                for p in range(NP):
                    gated(0, p)
                steps_b(step, dve)
                gate_y(NC - 1)
                out_resid(NC - 1)
                dve.wait_ge(m_res, NC)
                stats(norm_f2(NC - 1), X3)
                norm(norm_f2(NC - 1), X3)
                for p in range(NP):
                    gated(ffn_2(NC - 1), p)
                resid(f_out, ffn_2(NC - 1) + 1, X3, f_res)
    return nc


def kernel(**a):
    import numpy as np
    import concourse.bacc as bacc
    from concourse.bass_utils import run_bass_kernel_spmd

    ffn, mamba, rwkv = "L0_ffn_", "L0_attn_b_", "L0_attn_a_"
    x = np.asarray(a[rwkv + "x"])
    B, T, H = x.shape

    def columns(v):
        v = np.asarray(v)
        return np.moveaxis(v.reshape((-1, P) + v.shape[1:]), 0, 1)

    gate, up, down = (np.asarray(a[ffn + n]) for n in ("gate_idx", "up_idx", "down_idx"))
    inner = gate.shape[0]
    tiles = -(-inner // P)
    down = np.pad(down.T, ((0, tiles * P - inner), (0, 0)))
    idx = np.concatenate([columns(w).reshape(P, -1) for w in (gate.T, up.T, down)], axis=1)
    arrays = dict(
        x=x.reshape(B * T, H),
        w_rvk=np.asarray(a[rwkv + "W_rvk"]).T,
        w_out=np.asarray(a[rwkv + "W_out"]).T,
        decay=columns(a[rwkv + "time_decay"]),
        first=columns(a[rwkv + "time_first"]),
        idx=idx,
        lut=np.asarray(a[ffn + "lut"]),
        w_in=np.asarray(a[mamba + "in_proj_w"]).T,
        conv_w=columns(np.asarray(a[mamba + "conv_w"])[:, 0]),
        conv_b=columns(a[mamba + "conv_b"]),
        w_x=np.asarray(a[mamba + "x_proj_w"]).T,
        w_dt=np.asarray(a[mamba + "dt_proj_w"]).T,
        b_dt=columns(a[mamba + "dt_proj_b"]),
        a_log=columns(a[mamba + "A_log"]),
        d_skip=columns(a[mamba + "D_param"]),
        w_o=np.asarray(a[mamba + "out_proj_w"]).T,
    )
    arrays = {n: np.ascontiguousarray(v) for n, v in arrays.items()}
    nc = bacc.Bacc("TRN2", target_bir_lowering=False, num_devices=1)
    args = {n: nc.dram_tensor(n, v.shape, mybir.dt.from_np(v.dtype), kind="ExternalInput").ap() for n, v in arrays.items()}
    out = nc.dram_tensor("out", (B * T, H), F32, kind="ExternalOutput").ap()
    hybrid_block_kernel(nc, **args, inner=inner, out=out)
    r = run_bass_kernel_spmd(nc, [arrays], core_ids=[0])
    return np.asarray(r.results[0]["out"]).reshape(B, T, H)
```

```python
from contextlib import ExitStack

import concourse.bass as bass
from concourse import mybir

ALU = mybir.AluOpType
ACT = mybir.ActivationFunctionType
F32 = mybir.dt.float32
I32 = mybir.dt.int32

P = 128
CH = 256
TT = CH // P
EPS = 1e-5
FLOOR = -1e38
DEC = 520

G_SILU = (6, 9)
F1_EVAC = 12
F1_SILU = (15, 18, 21, 24, 27, 29)
F2_STAT = 3
F2_NORM = 29
F1_RES = 36
F2_EVAC = 38
F2_SILU = (43, 46, 49, 52, 55, 57)
MULT = -1
M_STAT = 58
M_NORM = 60
F2_RES = 64


def hybrid_block_kernel(
    nc, x, w_rvk, w_out, decay, first, idx, lut, w_in, conv_w, conv_b, w_x, w_dt, b_dt, a_log, d_skip, w_o, inner, out
):
    N, H = x.shape
    KH = H // P
    NC = N // CH
    SEQ = NC // 2
    E = w_in.shape[1] // 2
    ME = E // P
    S = a_log.shape[2]
    R = w_dt.shape[0]
    KC = conv_w.shape[2]
    IN = inner
    MI = -(-IN // P)
    LAST = IN - (MI - 1) * P
    GU = KH * IN
    WF = 2 * GU + MI * H
    PIECES = WF // DEC
    NP = (MI + 1) // 2
    NE = S * ME // 2
    assert WF == idx.shape[1] and WF % DEC == 0 and PIECES == 2 * NC and R == P and KC == 4

    def least(n):
        return max(n, 0) if isinstance(n, int) else n

    x_t = x.rearrange("(c t p) d -> c p t d", t=TT, p=P)
    out_t = out.rearrange("(c t p) d -> c p t d", t=TT, p=P)
    x1_d = nc.dram_tensor("x1_scratch", (N, H), F32, kind="Internal").ap().rearrange("(c t p) d -> c p t d", t=TT, p=P)
    x2_d = nc.dram_tensor("x2_scratch", (N, H), F32, kind="Internal").ap().rearrange("(c t p) d -> c p t d", t=TT, p=P)
    bc_d = nc.dram_tensor("bc_scratch", (NC, 2, S, CH), F32, kind="Internal").ap()

    with ExitStack() as ctx:
        sem = lambda name: ctx.enter_context(nc.semaphore(name))

        def buf(stack, name, shape, dt=F32):
            return stack.enter_context(nc.sbuf_tensor(name, [P] + shape, dt))

        wffn = buf(ctx, "wffn", [WF])
        wg = wffn[:, 0:GU].rearrange("p (k n) -> p k n", k=KH)
        wu = wffn[:, GU:2 * GU].rearrange("p (k n) -> p k n", k=KH)
        wd = wffn[:, 2 * GU:WF].rearrange("p (k n) -> p k n", k=MI)
        ident = buf(ctx, "ident", [P])
        keep = buf(ctx, "keep", [NC + 1])
        floor = buf(ctx, "floor", [NC + 1])
        mhalf = buf(ctx, "mhalf", [TT])
        bnst = buf(ctx, "bnst", [TT, 6])
        mv = buf(ctx, "mv", [TT, 2])
        veps = buf(ctx, "veps", [TT])
        tick = buf(ctx, "tick", [1])
        rstd = buf(ctx, "rstd", [TT])

        const_ready = sem("const_ready")
        ident_zero = sem("ident_zero")
        par_loaded = sem("par_loaded")
        x_loaded = [sem(f"x_loaded{s}") for s in range(2)]
        xr_loaded = sem("xr_loaded")
        x1_stored = sem("x1_stored")
        idx_loaded = [sem(f"idx_loaded{h}") for h in range(2)]
        dec_ready = sem("dec_ready")
        dec_step = sem("dec_step")
        dec_stored = [sem(f"dec_stored{h}") for h in range(2)]
        a_stat, a_var, a_veps, a_rstd, a_xn = sem("a_stat"), sem("a_var"), sem("a_veps"), sem("a_rstd"), sem("a_xn")
        a_tr, a_xnT, a_rvk, a_evac = sem("a_tr"), sem("a_xnT"), sem("a_rvk"), sem("a_evac")
        a_carry, a_o, a_z, a_dd, a_kko = sem("a_carry"), sem("a_o"), sem("a_z"), sem("a_dd"), sem("a_kko")
        a_eo, a_ek, a_kv, a_relu, a_mix, a_pq = sem("a_eo"), sem("a_ek"), sem("a_kv"), sem("a_relu"), sem("a_mix"), sem("a_pq")
        a_bv, a_old, a_num, a_den, a_nsig = sem("a_bv"), sem("a_old"), sem("a_num"), sem("a_den"), sem("a_nsig")
        a_ln, a_r0, a_nt, a_rec, a_y = sem("a_ln"), sem("a_r0"), sem("a_nt"), sem("a_rec"), sem("a_y")
        a_out, a_resid = sem("a_out"), sem("a_resid")
        setup_step = sem("setup_step")

        with ExitStack() as pa:
            wr = buf(pa, "wr", [KH, 3 * H])
            wo1 = buf(pa, "wo1", [KH, H])
            dec = buf(pa, "dec", [KH])
            fst = buf(pa, "fst", [KH])
            nfst = buf(pa, "nfst", [KH])
            lutS = buf(pa, "lutS", [16])
            lutX = buf(pa, "lutX", [8], I32)
            X = [buf(pa, f"X{s}", [TT, H]) for s in range(2)]
            XR = buf(pa, "XR", [TT, H])
            xn = buf(pa, "xn", [TT, H])
            xnT = buf(pa, "xnT", [KH, CH])
            sg = [buf(pa, f"sg{s}", [KH, CH]) for s in range(2)]
            vv = [buf(pa, f"vv{s}", [KH, CH]) for s in range(2)]
            kk = [buf(pa, f"kk{s}", [KH, CH]) for s in range(2)]
            oX = buf(pa, "oX", [KH, CH + 1])
            pX = buf(pa, "pX", [KH, CH + 1])
            qX = buf(pa, "qX", [KH, CH + 1])
            EO = buf(pa, "EO", [KH, CH])
            EK = buf(pa, "EK", [KH, CH])
            Z = buf(pa, "Z", [KH, CH])
            M = buf(pa, "M", [KH, CH])
            MA = buf(pa, "MA", [KH, CH])
            MB = buf(pa, "MB", [KH, CH])
            yT = buf(pa, "yT", [KH, CH])
            ix = [buf(pa, f"ix{s}", [DEC], I32) for s in range(2)]
            bit = [buf(pa, f"bit{b}", [DEC], I32) for b in range(4)]
            nA = [buf(pa, f"nA{s}", [DEC], I32) for s in range(2)]
            nB, nC, nE = (buf(pa, f"n{c}", [DEC], I32) for c in "BCE")
            trP = pa.enter_context(nc.psum_tensor("trP", [P, KH, CH], F32))
            rvkP = [pa.enter_context(nc.psum_tensor(f"rvkP{s}", [P, KH, CH], F32)) for s in range(2)]
            outP = pa.enter_context(nc.psum_tensor("outP", [P, TT, H], F32))
            block = pa.enter_context(nc.Block())

            def steps_a(step, eng):
                step(-1, 1, True, False)
                step(0, 0, True, True)
                step(1, 1, True, True)
                with eng.Fori(2, NC - 3, 2) as c:
                    step(c, 0, True, True)
                    step(c + 1, 1, True, True)
                step(NC - 2, 0, True, True)
                step(NC - 1, 1, False, True)

            @block.sync
            def _(sp):
                sp.dma_start(X[0][:], x_t[0]).then_inc(x_loaded[0], 16)
                sp.dma_start(wr[:], w_rvk.rearrange("(k p) n -> p k n", p=P)).then_inc(par_loaded, 16)
                sp.dma_start(dec[:], decay).then_inc(par_loaded, 16)
                sp.dma_start(fst[:], first).then_inc(par_loaded, 16)
                sp.dma_start(lutS[:], lut.partition_broadcast(P)).then_inc(par_loaded, 16)
                sp.dma_start(wo1[:], w_out.rearrange("(k p) n -> p k n", p=P)).then_inc(par_loaded, 16)
                sp.dma_start(X[1][:], x_t[1]).then_inc(x_loaded[1], 16)
                for q in range(2):
                    sp.dma_start(ix[q][:], idx[:, q * DEC:(q + 1) * DEC]).then_inc(idx_loaded[q], 16)

                def step(c, s, more_x, more_idx):
                    if more_x:
                        sp.wait_ge(a_xn, TT * (c + 1))
                        sp.wait_ge(par_loaded, 80)
                        sp.dma_start(X[s][:], x_t[c + 2]).then_inc(x_loaded[s], 16)
                    sp.wait_ge(x1_stored, 16 * c)
                    sp.wait_ge(par_loaded, 80)
                    sp.dma_start(XR[:], x_t[c]).then_inc(xr_loaded, 16)
                    for h in range(2):
                        q = 2 * c + h
                        sp.wait_ge(dec_ready, q + 1)
                        sp.wait_ge(par_loaded, 80)
                        sp.dma_start(wffn[:, bass.ds(q * DEC, DEC)], nA[h][:].bitcast(F32)).then_inc(dec_stored[h], 16)
                        if more_idx:
                            sp.dma_start(ix[h][:], idx[:, bass.ds((q + 2) * DEC, DEC)]).then_inc(idx_loaded[h], 16)
                    sp.wait_ge(a_resid, c + 1)
                    sp.wait_ge(par_loaded, 80)
                    sp.dma_start(x1_d[c], XR[:]).then_inc(x1_stored, 16)

                step(0, 0, True, True)
                step(1, 1, True, True)
                with sp.Fori(2, NC - 3, 2) as c:
                    step(c, 0, True, True)
                    step(c + 1, 1, True, True)
                step(NC - 2, 0, False, True)
                step(NC - 1, 1, False, False)
                sp.wait_ge(x1_stored, 16 * NC)
                for h in range(2):
                    sp.wait_ge(dec_stored[h], 16 * NC)

            @block.gpsimd
            def _(pool):
                nc.gpsimd.memset(ident[:], 0.0).then_inc(ident_zero, 1)
                nc.gpsimd.memset(mhalf[:], -0.5).then_inc(const_ready, 1)
                pool.wait_ge(ident_zero, 1)
                nc.gpsimd.affine_select(out=ident[:], in_=ident[:], compare_op=ALU.not_equal, fill=1.0, base=0,
                                        pattern=[[-1, P]], channel_multiplier=1).then_inc(const_ready, 1)
                pool.wait_ge(const_ready, 2)

                def step(c, s, front, back):
                    if front:
                        pool.wait_ge(a_veps, c + 2)
                        nc.gpsimd.tensor_tensor(rstd[:], veps[:], mhalf[:], ALU.pow).then_inc(a_rstd, 1)
                    if back:
                        pool.wait_ge(a_o, KH * (c + 1))
                        pool.wait_ge(a_pq, 2 * KH * c)
                        nc.gpsimd.tensor_tensor(EO[:], oX[:, :, 0:CH], oX[:, :, 1:CH + 1], ALU.subtract).then_inc(a_dd, 1)
                        nc.gpsimd.tensor_tensor(EK[:], kk[s][:], oX[:, :, 1:CH + 1], ALU.subtract).then_inc(a_kko, 1)
                        pool.wait_ge(a_y, c)
                        nc.gpsimd.tensor_tensor(Z[:], kk[s][:], oX[:, :, 0:CH], ALU.subtract).then_inc(a_z, 1)
                        pool.wait_ge(a_ek, c + 1)
                        pool.wait_ge(a_nt, c)
                        nc.gpsimd.tensor_tensor(M[:], EK[:], vv[s][:], ALU.mult).then_inc(a_kv, 1)
                        pool.wait_ge(a_mix, c + 1)
                        pool.wait_ge(a_kv, c + 1)
                        nc.gpsimd.tensor_tensor(vv[s][:], MB[:], vv[s][:], ALU.mult).then_inc(a_bv, 1)
                        pool.wait_ge(a_old, 2 * (c + 1))
                        pool.wait_ge(a_bv, c + 1)
                        nc.gpsimd.tensor_tensor(Z[:], Z[:], vv[s][:], ALU.add).then_inc(a_num, 1)
                        pool.wait_ge(a_num, c + 1)
                        nc.gpsimd.tensor_tensor(Z[:], Z[:], sg[s][:], ALU.mult).then_inc(a_nsig, 1)
                        pool.wait_ge(a_r0, c + 1)
                        nc.gpsimd.tensor_tensor(MB[:], M[:], MA[:], ALU.mult).then_inc(a_nt, 1)

                steps_a(step, pool)

            @block.scalar
            def _(act):
                act.wait_ge(par_loaded, 80)
                nc.scalar.activation(dec[:], dec[:], ACT.Exp).then_inc(setup_step, 1)

                def step(c, s, front, back):
                    f, sf = c + 1, 1 - s
                    if front:
                        act.wait_ge(a_tr, f + 1)
                        act.wait_ge(a_rvk, 3 * f)
                        nc.scalar.activation(xnT[:], trP[:], ACT.Copy).then_inc(a_xnT, 1)
                    if back:
                        act.wait_ge(a_dd, c + 1)
                        act.wait_ge(setup_step, 4)
                        for m in range(KH):
                            nc.scalar.activation(EO[:, m, :], EO[:, m, :], ACT.Exp, bias=dec[:, m:m + 1]).then_inc(a_eo, 1)
                        act.wait_ge(a_kko, c + 1)
                        nc.scalar.activation(EK[:], EK[:], ACT.Exp).then_inc(a_ek, 1)
                    if back:
                        act.wait_ge(a_z, c + 1)
                        act.wait_ge(a_y, c)
                        for m in range(KH):
                            nc.scalar.activation(MA[:, m, :], Z[:, m, :], ACT.Relu, bias=fst[:, m:m + 1]).then_inc(a_relu, 1)
                        for m in range(KH):
                            nc.scalar.activation(MB[:, m, :], Z[:, m, :], ACT.Relu, bias=nfst[:, m:m + 1], scale=-1.0).then_inc(a_relu, 1)
                        act.wait_ge(a_relu, 2 * KH * (c + 1))
                        nc.scalar.activation(MA[:], MA[:], ACT.Exp, scale=-1.0)
                        nc.scalar.activation(MB[:], MB[:], ACT.Exp, scale=-1.0).then_inc(a_mix, 1)
                    if front:
                        act.wait_ge(a_rvk, 3 * f + 1)
                        act.wait_ge(a_nsig, least(f - 1))
                        nc.scalar.activation(sg[sf][:], rvkP[sf][:], ACT.Sigmoid).then_inc(a_evac, 1)
                    if front:
                        act.wait_ge(a_rvk, 3 * f + 2)
                        act.wait_ge(a_num, least(f - 1))
                        nc.scalar.activation(vv[sf][:], rvkP[1 - sf][:], ACT.Copy).then_inc(a_evac, 1)
                    if back:
                        act.wait_ge(a_den, c + 1)
                        nc.scalar.activation(MA[:], M[:], ACT.Ln).then_inc(a_ln, 1)
                        act.wait_ge(a_ln, c + 1)
                        nc.scalar.activation(MA[:], MA[:], ACT.Exp, scale=-1.0).then_inc(a_r0, 1)
                    if front:
                        act.wait_ge(a_rvk, 3 * f + 3)
                        act.wait_ge(a_z, least(f - 1))
                        act.wait_ge(a_kko, least(f - 1))
                        nc.scalar.activation(kk[sf][:], rvkP[sf][:], ACT.Copy).then_inc(a_evac, 1)

                steps_a(step, act)

            @block.tensor
            def _(pe):
                pe.wait_ge(const_ready, 2)
                pe.wait_ge(par_loaded, 80)

                def step(c, s, front, back):
                    f, sf = c + 1, 1 - s
                    if front:
                        pe.wait_ge(a_xn, TT * (f + 1))
                        pe.wait_ge(a_xnT, f)
                        for k in range(KH):
                            for t in range(TT):
                                last = nc.tensor.transpose(trP[:, k, t * P:(t + 1) * P], xn[:, t, k * P:(k + 1) * P], ident[:])
                        last.then_inc(a_tr, 1)
                        pe.wait_ge(a_xnT, f + 1)
                        for g in range(3):
                            pe.wait_ge(a_evac, least(3 * f + g - 1))
                            for m in range(KH):
                                for k in range(KH):
                                    last = nc.tensor.matmul(rvkP[(sf + g) % 2][:, m, :], wr[:, k, g * H + m * P:g * H + (m + 1) * P],
                                                            xnT[:, k, :], start=(k == 0), stop=(k == KH - 1))
                            last.then_inc(a_rvk, 1)
                    if back:
                        pe.wait_ge(a_y, c + 1)
                        pe.wait_ge(a_resid, c)
                        for t in range(TT):
                            for k in range(KH):
                                last = nc.tensor.matmul(outP[:, t, :], yT[:, k, t * P:(t + 1) * P], wo1[:, k, :],
                                                        start=(k == 0), stop=(k == KH - 1))
                        last.then_inc(a_out, 1)

                steps_a(step, pe)

            @block.vector
            def _(dve):
                V = nc.vector
                V.memset(keep[:], 1.0)
                V.memset(floor[:], 0.0)
                for t in (oX, pX, qX):
                    V.memset(t[:, :, CH:CH + 1], 0.0)
                V.memset(veps[:], 1.0).then_inc(setup_step, 1)
                dve.wait_ge(setup_step, 2)
                V.memset(keep[:, 0:NC:SEQ], 0.0)
                V.memset(floor[:, 0:NC:SEQ], FLOOR)
                V.tensor_scalar(dec[:], dec[:], -1.0, None, ALU.mult).then_inc(setup_step, 1)
                lutI = lutS[:].bitcast(I32).rearrange("p (a b) -> p a b", b=2)
                V.tensor_tensor(lutX[:], lutI[:, :, 0], lutI[:, :, 1], ALU.bitwise_xor)
                V.tensor_scalar(nfst[:], fst[:], -1.0, None, ALU.mult).then_inc(setup_step, 1)
                dve.wait_ge(setup_step, 4)

                def alone(semaphore, count):
                    dve.wait_ge(semaphore, count)
                    V.memset(tick[:], 0.0)

                def decode(c, h):
                    q, a = 2 * c + h, nA[h]

                    def leaf(dst, j, k=0):
                        if k:
                            dve.wait_ge(dec_step, 18 * q + k)
                        return V.tensor_scalar(dst[:], bit[0][:], lutX[:, j:j + 1], lutI[:, j, 0:1], ALU.bitwise_and, ALU.bitwise_xor)

                    def pick(dst, b, src, k=0):
                        if k:
                            alone(dec_step, 18 * q + k)
                        return V.copy_predicated(dst[:], bit[b][:], src[:])

                    dve.wait_ge(idx_loaded[h], 16 * (c + 1))
                    dve.wait_ge(dec_ready, q)
                    V.tensor_scalar(bit[0][:], ix[h][:], 31, 31, ALU.logical_shift_left, ALU.arith_shift_right).then_inc(dec_step, 1)
                    for b in range(1, 4):
                        V.tensor_scalar(bit[b][:], ix[h][:], 1 << b, None, ALU.bitwise_and).then_inc(dec_step, 1)
                    dve.wait_ge(dec_stored[h], 16 * c)
                    dve.wait_ge(dec_step, 18 * q + 1)
                    leaf(a, 0).then_inc(dec_step, 1)
                    leaf(nB, 1).then_inc(dec_step, 1)
                    leaf(nC, 2, 6).then_inc(dec_step, 1)
                    pick(a, 1, nB).then_inc(dec_step, 1)
                    leaf(nB, 3, 8).then_inc(dec_step, 1)
                    leaf(nE, 4, 9).then_inc(dec_step, 1)
                    pick(nC, 1, nB).then_inc(dec_step, 1)
                    leaf(nB, 5, 11).then_inc(dec_step, 1)
                    pick(a, 2, nC).then_inc(dec_step, 1)
                    leaf(nC, 6, 13).then_inc(dec_step, 1)
                    pick(nE, 1, nB).then_inc(dec_step, 1)
                    leaf(nB, 7, 15).then_inc(dec_step, 1)
                    pick(nC, 1, nB, 16).then_inc(dec_step, 1)
                    pick(nE, 2, nC, 17).then_inc(dec_step, 1)
                    pick(a, 3, nE, 18).then_inc(dec_ready, 1)

                def resid(c):
                    dve.wait_ge(a_out, c + 1)
                    dve.wait_ge(xr_loaded, 16 * (c + 1))
                    V.tensor_tensor(XR[:], outP[:], XR[:], ALU.add).then_inc(a_resid, 1)

                def step(c, s, front, back):
                    f, sf = c + 1, 1 - s
                    if front:
                        dve.wait_ge(x_loaded[sf], 8 * (f - sf) + 16)
                        dve.wait_ge(a_var, TT * f)
                        for t in range(TT):
                            V.bn_stats(bnst[:, t, :], X[sf][:, t, :]).then_inc(a_stat, 1)
                        dve.wait_ge(a_xn, TT * f)
                        alone(a_stat, TT * (f + 1))
                        for t in range(TT):
                            V.bn_aggr(mv[:, t, :], bnst[:, t, :]).then_inc(a_var, 1)
                        dve.wait_ge(a_var, TT * (f + 1))
                        dve.wait_ge(a_rstd, f)
                        V.tensor_scalar(veps[:], mv[:, :, 1], EPS, None, ALU.add).then_inc(a_veps, 1)
                    if back:
                        dve.wait_ge(a_dd, c)
                        dve.wait_ge(a_old, 2 * c)
                        V.tensor_scalar(oX[:, :, 0:1], oX[:, :, CH:CH + 1], keep[:, bass.ds(c, 1)], floor[:, bass.ds(c, 1)],
                                        ALU.mult, ALU.add).then_inc(a_carry, 1)
                        V.tensor_scalar(pX[:, :, 0:1], pX[:, :, CH:CH + 1], keep[:, bass.ds(c, 1)], None, ALU.mult).then_inc(a_carry, 1)
                        V.tensor_scalar(qX[:, :, 0:1], qX[:, :, CH:CH + 1], keep[:, bass.ds(c, 1)], None, ALU.mult).then_inc(a_carry, 1)
                        dve.wait_ge(a_evac, 3 * (c + 1))
                        dve.wait_ge(a_carry, 3 * (c + 1))
                        for m in range(KH):
                            V.tensor_tensor_scan(oX[:, m, 1:CH + 1], dec[:, m:m + 1].to_broadcast([P, CH]), kk[s][:, m, :],
                                                 oX[:, m, 0:1], ALU.add, ALU.max).then_inc(a_o, 1)
                    if front:
                        dve.wait_ge(a_rstd, f + 1)
                        dve.wait_ge(a_tr, f)
                        for t in range(TT):
                            V.tensor_scalar(xn[:, t, :], X[sf][:, t, :], mv[:, t, 0:1], rstd[:, t:t + 1],
                                            ALU.subtract, ALU.mult).then_inc(a_xn, 1)
                    if back:
                        decode(c, 0)
                        dve.wait_ge(a_eo, KH * (c + 1))
                        dve.wait_ge(a_kv, c + 1)
                        for m in range(KH):
                            V.tensor_tensor_scan(pX[:, m, 1:CH + 1], EO[:, m, :], M[:, m, :], pX[:, m, 0:1], ALU.mult, ALU.add).then_inc(a_pq, 1)
                            V.tensor_tensor_scan(qX[:, m, 1:CH + 1], EO[:, m, :], EK[:, m, :], qX[:, m, 0:1], ALU.mult, ALU.add).then_inc(a_pq, 1)
                        if not (isinstance(c, int) and c == 0):
                            resid(c - 1)
                        dve.wait_ge(a_mix, c + 1)
                        dve.wait_ge(a_pq, 2 * KH * (c + 1))
                        dve.wait_ge(a_z, c + 1)
                        V.tensor_tensor(Z[:], MA[:], pX[:, :, 0:CH], ALU.mult).then_inc(a_old, 1)
                        V.tensor_tensor(M[:], MA[:], qX[:, :, 0:CH], ALU.mult).then_inc(a_old, 1)
                        dve.wait_ge(a_old, 2 * (c + 1))
                        V.tensor_tensor(M[:], M[:], MB[:], ALU.add).then_inc(a_den, 1)
                        decode(c, 1)
                        dve.wait_ge(a_nt, c + 1)
                        V.scalar_tensor_tensor(MB[:], MB[:], 2.0, MA[:], ALU.subtract, ALU.mult, reverse0=True).then_inc(a_rec, 1)
                        dve.wait_ge(a_rec, c + 1)
                        dve.wait_ge(a_nsig, c + 1)
                        dve.wait_ge(a_out, c)
                        V.tensor_tensor(yT[:], Z[:], MB[:], ALU.mult).then_inc(a_y, 1)

                steps_a(step, dve)
                resid(NC - 1)

        win = buf(ctx, "win", [KH, 2 * E])
        wx = buf(ctx, "wx", [ME, R + 2 * S])
        wdt = buf(ctx, "wdt", [E])
        wo = buf(ctx, "wo", [ME, H])
        cw = buf(ctx, "cw", [ME, KC])
        cb = buf(ctx, "cb", [ME])
        bdt = buf(ctx, "bdt", [ME])
        dsk = buf(ctx, "dsk", [ME])
        A = buf(ctx, "A", [ME, S])
        XM = buf(ctx, "XM", [TT, H])
        X3 = buf(ctx, "X3", [TT, H])
        nrm = buf(ctx, "nrm", [TT, H])
        nT = buf(ctx, "nT", [KH, CH])
        hT = buf(ctx, "hT", [MI, CH])
        U = buf(ctx, "U", [ME, CH])
        delta = buf(ctx, "delta", [ME, CH])
        yacc = buf(ctx, "yacc", [ME, CH])
        sgm = buf(ctx, "sgm", [ME, CH])
        bcS = buf(ctx, "bcS", [CH])
        dtl = buf(ctx, "dtl", [CH])
        xext = [buf(ctx, f"xext{s}", [2, CH + KC - 1]) for s in range(2)]
        cc = buf(ctx, "cc", [ME, KC - 1])
        hc = buf(ctx, "hc", [S, ME])
        BC = [buf(ctx, f"BC{s}", [2, CH]) for s in range(3)]
        dBu = [buf(ctx, f"dBu{s}", [2, CH]) for s in range(4)]
        prod = [buf(ctx, f"prod{s}", [2, CH]) for s in range(2)]
        W = [ctx.enter_context(nc.psum_tensor(f"W{s}", [P, 4, CH], F32)) for s in range(2)]
        D = ctx.enter_context(nc.psum_tensor("D", [P, ME, CH], F32))

        wts_loaded, small_loaded = sem("wts_loaded"), sem("small_loaded")
        b_setup = sem("b_setup")
        xm_loaded, x2_stored, x3_loaded, out_stored = sem("xm_loaded"), sem("x2_stored"), sem("x3_loaded"), sem("out_stored")
        bc_stored = sem("bc_stored")
        bc_loaded = [sem(f"bc_loaded{s}") for s in range(3)]
        n_stat, n_var, n_veps, n_rstd, n_done = sem("n_stat"), sem("n_var"), sem("n_veps"), sem("n_rstd"), sem("n_done")
        n_tr, n_T = sem("n_tr"), sem("n_T")
        f_gu, f_silu, f_h, f_out, f_res = sem("f_gu"), sem("f_silu"), sem("f_h"), sem("f_out"), sem("f_res")
        m_x, m_ext, m_tap, m_in, m_conv, m_cc = sem("m_x"), sem("m_ext"), sem("m_tap"), sem("m_in"), sem("m_conv"), sem("m_cc")
        m_u, m_skip, m_g, m_sg, m_bc, m_bcS = sem("m_u"), sem("m_skip"), sem("m_g"), sem("m_sg"), sem("m_bc"), sem("m_bcS")
        m_dt, m_dtl, m_dp, m_abs, m_relu = sem("m_dt"), sem("m_dtl"), sem("m_dp"), sem("m_abs"), sem("m_relu")
        m_exp, m_ln, m_delta, m_du = sem("m_exp"), sem("m_ln"), sem("m_delta"), sem("m_du")
        s_dA, s_dBu, s_scan, s_hc = sem("s_dA"), sem("s_dBu"), sem("s_scan"), sem("s_hc")
        s_prod, s_hC, s_acc = sem("s_prod"), sem("s_hC"), sem("s_acc")
        m_y, m_out, m_res = sem("m_y"), sem("m_out"), sem("m_res")

        norms, ffns, loads = [("F1", 0), ("F1", 1), ("M", 0)], [("F1", 0), ("F1", 1)], [("x1", 0)]
        for i in range(NC):
            norms += [("F1", i + 2)] * (i + 2 < NC) + [("F2", i - 1)] * (i > 0) + [("M", i + 1)] * (i + 1 < NC)
            ffns += [("F1", i + 2)] * (i + 2 < NC) + [("F2", i - 1)] * (i > 0)
            loads += [("x1", i + 2)] * (i + 2 < NC) + [("x2", i + 1)] * (i + 1 < NC)
        norms, ffns = norms + [("F2", NC - 1)], ffns + [("F2", NC - 1)]

        def number(order, kind, chunk):
            if isinstance(chunk, int):
                return order.index((kind, chunk))
            lo = {"F1": 3, "F2": 0, "M": 2, "x1": 3, "x2": 2}[kind]
            at = [order.index((kind, n)) for n in range(lo, lo + NC - 3)]
            step = at[1] - at[0]
            assert at == list(range(at[0], at[-1] + 1, step))
            return chunk * step + (at[0] - lo * step)

        norm_no = lambda kind, chunk: number(norms, kind, chunk)
        ffn_no = lambda kind, chunk: number(ffns, kind, chunk)
        load_no = lambda kind, chunk: number(loads, kind, chunk)

        def steps_b(step, eng):
            step(0, False, True, True)
            with eng.Fori(1, NC - 2) as i:
                step(i, True, True, True)
            step(NC - 2, True, False, True)
            step(NC - 1, True, False, False)

        def rows(p):
            return [(m, LAST if m == MI - 1 else P) for m in (2 * p, 2 * p + 1) if m < MI]

        with nc.Block() as block:
            @block.sync
            def _(sp):
                sp.dma_start(XM[:], x1_d[0]).then_inc(xm_loaded, 16)
                for t, d in ((A, a_log), (cw, conv_w), (cb, conv_b), (bdt, b_dt), (dsk, d_skip)):
                    sp.dma_start(t[:], d).then_inc(small_loaded, 16)
                sp.dma_start(X3[:], x1_d[1]).then_inc(x3_loaded, 16)
                sp.dma_start(win[:], w_in.rearrange("(k p) n -> p k n", p=P)).then_inc(wts_loaded, 16)
                sp.dma_start(wx[:], w_x.rearrange("(k p) n -> p k n", p=P)).then_inc(wts_loaded, 16)
                sp.dma_start(wdt[:], w_dt).then_inc(wts_loaded, 16)
                sp.dma_start(wo[:], w_o.rearrange("(k p) n -> p k n", p=P)).then_inc(wts_loaded, 16)
                def keep_x2(i, rows_=XM):
                    sp.wait_ge(f_res, ffn_no("F1", i) + 1)
                    sp.wait_ge(small_loaded, 80)
                    sp.dma_start(x2_d[i], rows_[:]).then_inc(x2_stored, 16)

                def load_x2(i, stored):
                    sp.wait_ge(x2_stored, 16 * stored)
                    sp.wait_ge(small_loaded, 80)
                    sp.dma_start(XM[:], x2_d[i]).then_inc(xm_loaded, 16)

                def step(i, back, f1, more):
                    if f1:
                        sp.wait_ge(n_done, TT * (norm_no("M", i) + 1))
                        sp.wait_ge(small_loaded, 80)
                        sp.dma_start(XM[:], x1_d[i + 2]).then_inc(xm_loaded, 16)
                    sp.wait_ge(m_bcS, i + 1)
                    sp.wait_ge(small_loaded, 80)
                    sp.dma_start(bc_d[i].rearrange("a n t -> (a n) t"), bcS[0:2 * S, :]).then_inc(bc_stored, 16)
                    sp.wait_ge(bc_stored, 16 * (i + 1))
                    sp.wait_ge(small_loaded, 80)
                    for n in range(S):
                        if n >= 3:
                            sp.wait_ge(s_prod, NE * i + 4 * (n - 2))
                            sp.wait_ge(small_loaded, 80)
                        sp.dma_start(BC[n % 3][:], bc_d[i][:, n, :].partition_broadcast(P)).then_inc(bc_loaded[n % 3], 16)
                        if n == 10 and f1:
                            keep_x2(i + 2)
                        if n == 12 and more:
                            load_x2(i + 1, i + 3 if f1 else NC)
                    if back:
                        sp.wait_ge(f_res, ffn_no("F2", i - 1) + 1)
                        sp.wait_ge(small_loaded, 80)
                        sp.dma_start(out_t[i - 1], X3[:]).then_inc(out_stored, 16)
                        sp.wait_ge(out_stored, 16 * i)
                        sp.wait_ge(small_loaded, 80)
                    sp.dma_start(X3[:], x2_d[i]).then_inc(x3_loaded, 16)

                keep_x2(0)
                keep_x2(1, X3)
                sp.wait_ge(x2_stored, 32)
                steps_b(step, sp)
                sp.wait_ge(f_res, ffn_no("F2", NC - 1) + 1)
                sp.dma_start(out_t[NC - 1], X3[:]).then_inc(out_stored, 16)
                sp.wait_ge(out_stored, 16 * NC)

            @block.gpsimd
            def _(pool):
                def root(L):
                    pool.wait_ge(n_veps, L + 1)
                    pool.wait_ge(n_done, TT * L)
                    nc.gpsimd.tensor_tensor(rstd[:], veps[:], mhalf[:], ALU.pow).then_inc(n_rstd, 1)

                def step(i, back, f1, more):
                    if f1:
                        root(norm_no("F1", i + 2))

                    def outer(e):
                        n, j = divmod(e, 4)
                        slot = n % 3
                        if j == 0:
                            pool.wait_ge(bc_loaded[slot], 16 * ((6 if slot == 0 else 5) * i + n // 3 + 1))
                        if e in (0, 2):
                            pool.wait_ge(m_du, 2 * i + e // 2 + 1)
                        elif e >= 4:
                            pool.wait_ge(s_scan, 2 * NE * i + 2 * (e - 3))
                        nc.gpsimd.tensor_tensor(dBu[e % 4][:], U[:, 2 * j:2 * j + 2, :], BC[slot][:, 0:1, :].to_broadcast([P, 2, CH]),
                                                ALU.mult).then_inc(s_dBu, 1)

                    def add(e):
                        n, j = divmod(e, 4)
                        r = 3 * n + j
                        pool.wait_ge(s_prod, NE * i + e + 1)
                        if r == 0:
                            pool.wait_ge(m_skip, ME * (i + 1))
                        if r >= 3:
                            pool.wait_ge(s_acc, 3 * S * i + r - 2)
                        y = yacc[:, 2 * j:2 * j + 2, :]
                        nc.gpsimd.tensor_tensor(y, y, prod[r % 2][:], ALU.add).then_inc(s_acc, 1)

                    for e in range(4):
                        outer(e)
                    for e in range(NE):
                        if e + 4 < NE:
                            outer(e + 4)
                        if e % 4 < 3:
                            add(e)
                        if back and e == F2_STAT:
                            root(norm_no("F2", i - 1))
                        if more and e == M_STAT:
                            root(norm_no("M", i + 1))

                for L in range(3):
                    root(L)
                steps_b(step, pool)
                root(norm_no("F2", NC - 1))

            @block.scalar
            def _(act):
                N_ = nc.scalar

                def evac(L):
                    act.wait_ge(n_tr, L + 1)
                    N_.activation(nT[:], W[0][:], ACT.Copy).then_inc(n_T, 1)

                def silu(F, L, p):
                    act.wait_ge(f_gu, NP * F + p + 1)
                    if p < 2:
                        act.wait_ge(n_tr, L + 1)
                    else:
                        act.wait_ge(f_h, NP * F + p - 1)
                    r = rows(p)
                    w = len(r) * CH
                    N_.activation(nrm[0:r[0][1], p % 2, 0:w], W[1 - p % 2][0:r[0][1], 0:len(r), :].rearrange("p a t -> p (a t)"),
                                  ACT.Silu).then_inc(f_silu, 1)

                def step(i, back, f1, more):
                    for q in range(ME // 2):
                        act.wait_ge(m_x, 2 * i + q // 2 + 1)
                        act.wait_ge(m_cc, 4 * i + max(q - 1, 0))
                        act.wait_ge(m_conv, 24 * i + 6 * max(q - 1, 0))
                        src = W[1 - q // 2]
                        a = 2 * (q % 2)
                        N_.activation(xext[q % 2][:, :, KC - 1:], src[:, a:a + 2, :], ACT.Copy).then_inc(m_ext, 1)
                        act.wait_ge(s_dBu, NE * i)
                        for h in range(2):
                            m = 2 * q + h
                            N_.activation(U[:, m, :], src[:, a + h, :], ACT.Identity, bias=cb[:, m:m + 1],
                                          scale=cw[:, m, KC - 1:KC]).then_inc(m_tap, 1)
                    for q in range(ME // 2):
                        act.wait_ge(m_conv, 24 * i + 6 * (q + 1))
                        N_.activation(U[:, 2 * q:2 * q + 2, :], U[:, 2 * q:2 * q + 2, :], ACT.Silu).then_inc(m_u, 1)
                    act.wait_ge(m_dt, i + 1)
                    N_.activation(dtl[:], W[1][:, 0, :], ACT.Copy).then_inc(m_dtl, 1)
                    act.wait_ge(m_bc, i + 1)
                    act.wait_ge(bc_stored, 16 * i)
                    N_.activation(bcS[0:2 * S, :], W[1][0:2 * S, 2, :], ACT.Copy).then_inc(m_bcS, 1)
                    act.wait_ge(m_u, 4 * (i + 1))
                    act.wait_ge(m_y, 2 * i)
                    for m in range(ME):
                        N_.activation(yacc[:, m, :], U[:, m, :], ACT.Identity, scale=dsk[:, m:m + 1]).then_inc(m_skip, 1)
                    act.wait_ge(s_prod, NE * i)
                    for h in range(2):
                        quad = slice(4 * h, 4 * h + 4)
                        act.wait_ge(m_dp, 2 * i + h + 1)
                        for m in range(4 * h, 4 * h + 4):
                            N_.activation(D[:, m, :], W[h][:, m % 4, :], ACT.Abs, bias=bdt[:, m:m + 1]).then_inc(m_abs, 1)
                        act.wait_ge(m_abs, ME * i + 4 * (h + 1))
                        N_.activation(D[:, quad, :], D[:, quad, :], ACT.Exp, scale=-1.0).then_inc(m_exp, 1)
                        act.wait_ge(m_exp, 2 * i + h + 1)
                        N_.activation(D[:, quad, :], D[:, quad, :], ACT.Ln, bias=1.0).then_inc(m_ln, 1)
                    for e in range(NE):
                        n, j = divmod(e, 4)
                        if e >= 4:
                            act.wait_ge(s_prod, NE * i + e - 3)
                        elif e % 2 == 0:
                            act.wait_ge(m_delta, 2 * i + e // 2 + 1)
                        for m in (2 * j, 2 * j + 1):
                            N_.activation(D[:, m, :], delta[:, m, :], ACT.Exp, scale=A[:, m, n:n + 1]).then_inc(s_dA, 1)
                        for h in range(2):
                            if e == G_SILU[h]:
                                act.wait_ge(m_g, 2 * i + h + 1)
                                act.wait_ge(m_out, i)
                                N_.activation(sgm[:, 4 * h:4 * h + 4, :], W[1 - h][:], ACT.Silu).then_inc(m_sg, 1)
                        if f1 and e == F1_EVAC:
                            evac(norm_no("F1", i + 2))
                        if back and e == F2_EVAC:
                            evac(norm_no("F2", i - 1))
                        for p in range(NP):
                            if f1 and e == F1_SILU[p]:
                                silu(ffn_no("F1", i + 2), norm_no("F1", i + 2), p)
                            if back and e == F2_SILU[p]:
                                silu(ffn_no("F2", i - 1), norm_no("F2", i - 1), p)
                    if more:
                        evac(norm_no("M", i + 1))

                act.wait_ge(small_loaded, 80)
                N_.activation(A[:], A[:], ACT.Exp).then_inc(b_setup, 1)
                for n in range(2):
                    evac(n)
                    for p in range(NP):
                        silu(n, n, p)
                evac(2)
                act.wait_ge(b_setup, 3)
                steps_b(step, act)
                evac(norm_no("F2", NC - 1))
                for p in range(NP):
                    silu(ffn_no("F2", NC - 1), norm_no("F2", NC - 1), p)

            @block.tensor
            def _(pe):
                T_ = nc.tensor

                def chain(dst, terms):
                    for n, (lhsT, rhs) in enumerate(terms):
                        last = T_.matmul(dst, lhsT, rhs, start=(n == 0), stop=(n == len(terms) - 1))
                    return last

                def turn(L):
                    pe.wait_ge(n_done, TT * (L + 1))
                    for k in range(KH):
                        for t in range(TT):
                            last = T_.transpose(W[0][:, k, t * P:(t + 1) * P], nrm[:, t, k * P:(k + 1) * P], ident[:])
                    last.then_inc(n_tr, 1)

                def ffn(F, L):
                    for p in range(NP):
                        Wp = W[1 - p % 2]
                        if p < 2:
                            pe.wait_ge(n_T, L + 1)
                        else:
                            pe.wait_ge(f_h, NP * F + p - 1)
                        for half, wt in ((0, wg), (2, wu)):
                            for m, r in rows(p):
                                last = chain(Wp[0:r, half + m % 2, :], [(wt[:, k, m * P:m * P + r], nT[:, k, :]) for k in range(KH)])
                        last.then_inc(f_gu, 1)
                    pe.wait_ge(f_h, NP * F + NP - 1)
                    o = W[1][:].rearrange("p (t a) n -> p t (a n)", t=TT)
                    for t in range(TT):
                        for k in range(MI - 1):
                            T_.matmul(o[:, t, :], hT[:, k, t * P:(t + 1) * P], wd[:, k, :], start=(k == 0), stop=False)
                    pe.wait_ge(f_h, NP * F + NP)
                    for t in range(TT):
                        last = T_.matmul(o[:, t, :], hT[0:LAST, MI - 1, t * P:(t + 1) * P], wd[0:LAST, MI - 1, :], start=False, stop=True)
                    last.then_inc(f_out, 1)

                def project(i, Wp):
                    pe.wait_ge(m_y, 2 * (i + 1))
                    for t in range(TT):
                        last = chain(Wp[:].rearrange("p (t a) n -> p t (a n)", t=TT)[:, t, :],
                                     [(sgm[:, k, t * P:(t + 1) * P], wo[:, k, :]) for k in range(ME)])
                    last.then_inc(m_out, 1)

                def first_product(i, free0, free1):
                    pe.wait_ge(*free0)
                    turn(norm_no("M", i))
                    pe.wait_ge(*free1)
                    pe.wait_ge(n_T, norm_no("M", i) + 1)
                    for h in range(2):
                        for m in range(4 * h, 4 * h + 4):
                            last = chain(W[1 - h][:, m % 4, :], [(win[:, k, m * P:(m + 1) * P], nT[:, k, :]) for k in range(KH)])
                        last.then_inc(m_x, 1)

                def whole_ffn(kind, i, free0, free1):
                    F, L = ffn_no(kind, i), norm_no(kind, i)
                    pe.wait_ge(*free0)
                    turn(L)
                    pe.wait_ge(*free1)
                    ffn(F, L)
                    return (f_h, NP * (F + 1)), (f_res, F + 1)

                def step(i, back, f1, more):
                    for k in range(ME):
                        if k % 2 == 0:
                            pe.wait_ge(m_u, 4 * i + k // 2 + 1)
                        last = T_.matmul(W[1][:, 0, :], wx[:, k, 0:R], U[:, k, :], start=(k == 0), stop=(k == ME - 1))
                    last.then_inc(m_dt, 1)
                    chain(W[1][0:2 * S, 2, :], [(wx[:, k, R:R + 2 * S], U[:, k, :]) for k in range(ME)]).then_inc(m_bc, 1)
                    pe.wait_ge(m_dtl, i + 1)
                    for h in range(2):
                        if h == 1:
                            pe.wait_ge(m_bcS, i + 1)
                        for m in range(4 * h, 4 * h + 4):
                            last = chain(W[h][:, m % 4, :], [(wdt[:, m * P:(m + 1) * P], dtl[:])])
                        last.then_inc(m_dp, 1)
                    pe.wait_ge(m_relu, ME * i + 4)
                    if back:
                        project(i - 1, W[0])
                    for h in range(2):
                        if h == 0:
                            pe.wait_ge(m_relu, ME * (i + 1))
                        else:
                            pe.wait_ge(m_res, i)
                        for m in range(4 * h, 4 * h + 4):
                            last = chain(W[1 - h][:, m % 4, :], [(win[:, k, E + m * P:E + (m + 1) * P], nT[:, k, :]) for k in range(KH)])
                        last.then_inc(m_g, 1)
                    free = (m_sg, 2 * i + 2), (m_sg, 2 * i + 1)
                    if f1:
                        free = whole_ffn("F1", i + 2, *free)
                    if back:
                        free = whole_ffn("F2", i - 1, *free)
                    if more:
                        first_product(i + 1, *free)

                turn(0)
                ffn(0, 0)
                free = whole_ffn("F1", 1, (f_h, NP), (f_res, 1))
                pe.wait_ge(wts_loaded, 64)
                first_product(0, *free)
                steps_b(step, pe)
                F = ffn_no("F2", NC - 2)
                pe.wait_ge(f_res, F + 1)
                project(NC - 1, W[1])
                whole_ffn("F2", NC - 1, (f_h, NP * (F + 1)), (m_res, NC))

            @block.vector
            def _(dve):
                V = nc.vector

                def alone(semaphore, count):
                    dve.wait_ge(semaphore, count)
                    V.memset(tick[:], 0.0)

                def stats(L, rows_):
                    dve.wait_ge(n_done, TT * L)
                    for t in range(TT):
                        V.bn_stats(bnst[:, t, :], rows_[:, t, :]).then_inc(n_stat, 1)
                    alone(n_stat, TT * (L + 1))
                    for t in range(TT):
                        V.bn_aggr(mv[:, t, :], bnst[:, t, :]).then_inc(n_var, 1)
                    dve.wait_ge(n_var, TT * (L + 1))
                    V.tensor_scalar(veps[:], mv[:, :, 1], EPS, None, ALU.add).then_inc(n_veps, 1)

                def norm(L, rows_):
                    dve.wait_ge(n_rstd, L + 1)
                    for t in range(TT):
                        V.tensor_scalar(nrm[:, t, :], rows_[:, t, :], mv[:, t, 0:1], rstd[:, t:t + 1],
                                        ALU.subtract, ALU.mult).then_inc(n_done, 1)

                def gated(F, p):
                    dve.wait_ge(f_silu, NP * F + p + 1)
                    if p == 0:
                        dve.wait_ge(f_out, F)
                    r = rows(p)
                    n, w = r[0][1], len(r)
                    V.tensor_tensor(hT[0:n, 2 * p:2 * p + w, :], nrm[0:n, p % 2, 0:w * CH].rearrange("p (a t) -> p a t", a=w),
                                    W[1 - p % 2][0:n, 2:2 + w, :], ALU.mult).then_inc(f_h, 1)

                def resid(ready, count, rows_, done, Wp=W[1]):
                    dve.wait_ge(ready, count)
                    V.tensor_tensor(rows_[:].rearrange("p t d -> p (t d)"), Wp[:].rearrange("p a n -> p (a n)"),
                                    rows_[:].rearrange("p t d -> p (t d)"), ALU.add).then_inc(done, 1)

                def gate_y(i):
                    dve.wait_ge(s_acc, 3 * S * (i + 1))
                    dve.wait_ge(s_prod, NE * (i + 1))
                    dve.wait_ge(m_sg, 2 * (i + 1))
                    for h in range(2):
                        g = sgm[:, 4 * h:4 * h + 4, :]
                        V.tensor_tensor(g, yacc[:, 4 * h:4 * h + 4, :], g, ALU.mult).then_inc(m_y, 1)

                def out_resid(i, Wp=W[0]):
                    dve.wait_ge(x3_loaded, 16 * (i + 2))
                    resid(m_out, i + 1, X3, m_res, Wp)

                def conv(i, q):
                    x_ = xext[q % 2]
                    cq = cc[:, 2 * q:2 * q + 2, :]
                    dve.wait_ge(m_conv, 24 * i + 6 * max(q - 1, 0))
                    dve.wait_ge(m_cc, 4 * i + max(q - 1, 0))
                    V.tensor_copy(x_[:, :, 0:KC - 1], cq).then_inc(m_in, 1)
                    dve.wait_ge(m_tap, ME * i + 2 * q + 2)
                    dve.wait_ge(m_in, 4 * i + q + 1)
                    for k in range(KC - 1):
                        for h in range(2):
                            m = 2 * q + h
                            if k:
                                dve.wait_ge(m_conv, 24 * i + 6 * q + 2 * (k - 1) + h + 1)
                            V.scalar_tensor_tensor(U[:, m, :], x_[:, h, k:k + CH], cw[:, m, k:k + 1], U[:, m, :],
                                                   ALU.mult, ALU.add).then_inc(m_conv, 1)
                    V.tensor_scalar(cq, x_[:, :, CH:CH + KC - 1], keep[:, bass.ds(i + 1, 1)], None, ALU.mult).then_inc(m_cc, 1)

                def step(i, back, f1, more):
                    for q in range(ME // 2):
                        conv(i, q)
                    if f1:
                        dve.wait_ge(xm_loaded, 16 * (load_no("x1", i + 2) + 1))
                        stats(norm_no("F1", i + 2), XM)
                        dve.wait_ge(n_tr, norm_no("M", i) + 1)
                        norm(norm_no("F1", i + 2), XM)
                    dve.wait_ge(s_dA, 2 * NE * i)
                    for m in range(ME):
                        dve.wait_ge(m_abs, ME * i + (4 if m < 4 else 8))
                        V.tensor_scalar(delta[:, m, :], W[m // 4][:, m % 4, :], bdt[:, m:m + 1], 0.0, ALU.add, ALU.max).then_inc(m_relu, 1)
                    for h in range(2):
                        quad = slice(4 * h, 4 * h + 4)
                        dve.wait_ge(m_ln, 2 * i + h + 1)
                        dve.wait_ge(m_relu, ME * i + 4 * (h + 1))
                        V.tensor_tensor(delta[:, quad, :], delta[:, quad, :], D[:, quad, :], ALU.add).then_inc(m_delta, 1)
                        dve.wait_ge(m_skip, ME * (i + 1))
                        dve.wait_ge(m_bc, i + 1)
                        dve.wait_ge(m_delta, 2 * i + h + 1)
                        V.tensor_tensor(U[:, quad, :], U[:, quad, :], delta[:, quad, :], ALU.mult).then_inc(m_du, 1)

                    def scan(e, m):
                        dve.wait_ge(s_dA, 2 * NE * i + 2 * e + 2)
                        dve.wait_ge(s_dBu, NE * i + e + 1)
                        dve.wait_ge(s_hc, NE * i)
                        n = e // 4
                        V.tensor_tensor_scan(D[:, m, :], D[:, m, :], dBu[e % 4][:, m % 2, :], hc[:, n, m:m + 1],
                                             ALU.mult, ALU.add).then_inc(s_scan, 1)

                    def save(e):
                        n, j = divmod(e, 4)
                        dve.wait_ge(s_scan, 2 * NE * i + 2 * e + 2)
                        V.tensor_scalar(hc[:, n, 2 * j:2 * j + 2], D[:, 2 * j:2 * j + 2, CH - 1], keep[:, bass.ds(i + 1, 1)], None,
                                        ALU.mult).then_inc(s_hc, 1)

                    def times_c(e):
                        n, j = divmod(e, 4)
                        h_, r = D[:, 2 * j:2 * j + 2, :], 3 * n + j
                        c_ = BC[n % 3][:, 1:2, :].to_broadcast([P, 2, CH])
                        dve.wait_ge(bc_loaded[n % 3], 16 * ((6 if n % 3 == 0 else 5) * i + n // 3 + 1))
                        if j < 3:
                            dve.wait_ge(s_acc, 3 * S * i + max(r - 1, 0))
                            V.tensor_tensor(prod[r % 2][:], h_, c_, ALU.mult).then_inc(s_prod, 1)
                        else:
                            dve.wait_ge(s_hc, NE * i + e + 1)
                            V.tensor_tensor(h_, h_, c_, ALU.mult).then_inc(s_hC, 1)

                    def add(e):
                        dve.wait_ge(m_skip, ME * (i + 1))
                        dve.wait_ge(s_prod, NE * i + e - 3)
                        dve.wait_ge(s_hC, S * i + e // 4 + 1)
                        V.tensor_tensor(yacc[:, 6:8, :], D[:, 6:8, :], yacc[:, 6:8, :], ALU.add).then_inc(s_prod, 1)

                    for e in range(NE + 4):
                        j = e % 4
                        if e < NE:
                            scan(e, 2 * j)
                        if 1 <= e <= NE:
                            save(e - 1)
                        if e < NE:
                            scan(e, 2 * j + 1)
                        if 2 <= e <= NE + 1 and (e - 2) % 4 == 3:
                            add(e - 2)
                        if 1 <= e <= NE:
                            times_c(e - 1)
                        if e == NE + 1:
                            gate_y(i)
                        if back and e == F2_STAT:
                            out_resid(i - 1)
                            dve.wait_ge(m_res, i)
                            stats(norm_no("F2", i - 1), X3)
                        if back and e == F2_NORM:
                            if f1:
                                dve.wait_ge(f_h, NP * (ffn_no("F1", i + 2) + 1))
                            else:
                                dve.wait_ge(n_tr, norm_no("M", i) + 1)
                            norm(norm_no("F2", i - 1), X3)
                        for p in range(NP):
                            if f1 and e == F1_SILU[p] + MULT:
                                gated(ffn_no("F1", i + 2), p)
                            if back and e == F2_SILU[p] + MULT:
                                gated(ffn_no("F2", i - 1), p)
                        if f1 and e == F1_RES:
                            resid(f_out, ffn_no("F1", i + 2) + 1, XM, f_res)
                        if back and e == F2_RES:
                            resid(f_out, ffn_no("F2", i - 1) + 1, X3, f_res)
                        if more and e == M_STAT:
                            dve.wait_ge(xm_loaded, 16 * (load_no("x2", i + 1) + 1))
                            stats(norm_no("M", i + 1), XM)
                        if more and e == M_NORM:
                            if back:
                                dve.wait_ge(f_h, NP * (ffn_no("F2", i - 1) + 1))
                            else:
                                dve.wait_ge(f_h, NP * (ffn_no("F1", i + 2) + 1))
                            norm(norm_no("M", i + 1), XM)

                V.memset(hc[:], 0.0)
                V.memset(cc[:], 0.0).then_inc(b_setup, 1)
                dve.wait_ge(b_setup, 2)
                V.tensor_scalar(A[:], A[:], -1.0, None, ALU.mult).then_inc(b_setup, 1)
                dve.wait_ge(xm_loaded, 16)
                stats(0, XM)
                norm(0, XM)
                for n, rows_ in ((0, XM), (1, X3)):
                    for p in range(NP):
                        gated(n, p)
                    if n == 0:
                        dve.wait_ge(x3_loaded, 16)
                        stats(1, X3)
                        dve.wait_ge(f_h, NP)
                        norm(1, X3)
                    resid(f_out, n + 1, rows_, f_res)
                dve.wait_ge(f_h, 2 * NP)
                dve.wait_ge(f_res, 1)
                stats(2, XM)
                norm(2, XM)
                steps_b(step, dve)
                out_resid(NC - 1, W[1])
                L, F = norm_no("F2", NC - 1), ffn_no("F2", NC - 1)
                dve.wait_ge(m_res, NC)
                dve.wait_ge(f_h, NP * F)
                stats(L, X3)
                norm(L, X3)
                for p in range(NP):
                    gated(F, p)
                resid(f_out, F + 1, X3, f_res)
    return nc


def kernel(**a):
    import numpy as np
    import concourse.bacc as bacc
    from concourse.bass_utils import run_bass_kernel_spmd

    ffn, mamba, rwkv = "L0_ffn_", "L0_attn_b_", "L0_attn_a_"
    x = np.asarray(a[rwkv + "x"])
    B, T, H = x.shape

    def columns(v):
        v = np.asarray(v)
        return np.moveaxis(v.reshape((-1, P) + v.shape[1:]), 0, 1)

    gate, up, down = (np.asarray(a[ffn + n]) for n in ("gate_idx", "up_idx", "down_idx"))
    inner = gate.shape[0]
    tiles = -(-inner // P)
    down = np.pad(down.T, ((0, tiles * P - inner), (0, 0)))
    idx = np.concatenate([columns(w).reshape(P, -1) for w in (gate.T, up.T, down)], axis=1)
    arrays = dict(
        x=x.reshape(B * T, H),
        w_rvk=np.asarray(a[rwkv + "W_rvk"]).T,
        w_out=np.asarray(a[rwkv + "W_out"]).T,
        decay=columns(a[rwkv + "time_decay"]),
        first=columns(a[rwkv + "time_first"]),
        idx=idx,
        lut=np.asarray(a[ffn + "lut"]),
        w_in=np.asarray(a[mamba + "in_proj_w"]).T,
        conv_w=columns(np.asarray(a[mamba + "conv_w"])[:, 0]),
        conv_b=columns(a[mamba + "conv_b"]),
        w_x=np.asarray(a[mamba + "x_proj_w"]).T,
        w_dt=np.asarray(a[mamba + "dt_proj_w"]).T,
        b_dt=columns(a[mamba + "dt_proj_b"]),
        a_log=columns(a[mamba + "A_log"]),
        d_skip=columns(a[mamba + "D_param"]),
        w_o=np.asarray(a[mamba + "out_proj_w"]).T,
    )
    arrays = {n: np.ascontiguousarray(v) for n, v in arrays.items()}
    nc = bacc.Bacc("TRN2", target_bir_lowering=False, num_devices=1)
    args = {n: nc.dram_tensor(n, v.shape, mybir.dt.from_np(v.dtype), kind="ExternalInput").ap() for n, v in arrays.items()}
    out = nc.dram_tensor("out", (B * T, H), F32, kind="ExternalOutput").ap()
    hybrid_block_kernel(nc, **args, inner=inner, out=out)
    r = run_bass_kernel_spmd(nc, [arrays], core_ids=[0])
    return np.asarray(r.results[0]["out"]).reshape(B, T, H)
```

```python
from contextlib import ExitStack

import concourse.bass as bass
from concourse import mybir

ALU = mybir.AluOpType
ACT = mybir.ActivationFunctionType
F32 = mybir.dt.float32
I32 = mybir.dt.int32

P = 128
CH = 256
TT = CH // P
EPS = 1e-5
FLOOR = -1e38
DEC = 520

FILL = 4
TURN_AT = 6
G_SILU = (2, 5)
F1_EVAC = 8
F1_SILU = (13, 16, 19, 22, 25, 27)
F2_STAT = 2
F2_NORM = 27
F1_RES = 35
F2_EVAC = 36
F2_SILU = (40, 43, 46, 49, 52, 54)
MULT = -1
M_STAT = 55
M_NORM = 57
F2_RES = 61


def hybrid_block_kernel(
    nc, x, w_rvk, w_out, decay, first, idx, lut, w_in, conv_w, conv_b, w_x, w_dt, b_dt, a_log, d_skip, w_o, inner, out
):
    N, H = x.shape
    KH = H // P
    NC = N // CH
    SEQ = NC // 2
    E = w_in.shape[1] // 2
    ME = E // P
    S = a_log.shape[2]
    R = w_dt.shape[0]
    KC = conv_w.shape[2]
    IN = inner
    MI = -(-IN // P)
    LAST = IN - (MI - 1) * P
    GU = KH * IN
    WF = 2 * GU + MI * H
    PIECES = WF // DEC
    NP = (MI + 1) // 2
    NE = S * ME // 2
    assert WF == idx.shape[1] and WF % DEC == 0 and PIECES == 2 * NC and R == P and KC == 4

    def least(n):
        return max(n, 0) if isinstance(n, int) else n

    x_t = x.rearrange("(c t p) d -> c p t d", t=TT, p=P)
    out_t = out.rearrange("(c t p) d -> c p t d", t=TT, p=P)
    x1_d = nc.dram_tensor("x1_scratch", (N, H), F32, kind="Internal").ap().rearrange("(c t p) d -> c p t d", t=TT, p=P)
    x2_d = nc.dram_tensor("x2_scratch", (N, H), F32, kind="Internal").ap().rearrange("(c t p) d -> c p t d", t=TT, p=P)
    bc_d = nc.dram_tensor("bc_scratch", (NC, 2, S, CH), F32, kind="Internal").ap()

    with ExitStack() as ctx:
        sem = lambda name: ctx.enter_context(nc.semaphore(name))

        def buf(stack, name, shape, dt=F32):
            return stack.enter_context(nc.sbuf_tensor(name, [P] + shape, dt))

        wffn = buf(ctx, "wffn", [WF])
        wg = wffn[:, 0:GU].rearrange("p (k n) -> p k n", k=KH)
        wu = wffn[:, GU:2 * GU].rearrange("p (k n) -> p k n", k=KH)
        wd = wffn[:, 2 * GU:WF].rearrange("p (k n) -> p k n", k=MI)
        ident = buf(ctx, "ident", [P])
        keep = buf(ctx, "keep", [NC + 1])
        floor = buf(ctx, "floor", [NC + 1])
        mhalf = buf(ctx, "mhalf", [TT])
        bnst = buf(ctx, "bnst", [TT, 6])
        mv = buf(ctx, "mv", [TT, 2])
        veps = buf(ctx, "veps", [TT])
        tick = buf(ctx, "tick", [1])
        rstd = buf(ctx, "rstd", [TT])

        const_ready = sem("const_ready")
        ident_zero = sem("ident_zero")
        par_loaded = sem("par_loaded")
        x_loaded = [sem(f"x_loaded{s}") for s in range(2)]
        xr_loaded = sem("xr_loaded")
        x1_stored = sem("x1_stored")
        idx_loaded = [sem(f"idx_loaded{h}") for h in range(2)]
        dec_ready = sem("dec_ready")
        dec_step = sem("dec_step")
        dec_stored = [sem(f"dec_stored{h}") for h in range(2)]
        a_stat, a_var, a_veps, a_rstd, a_xn = sem("a_stat"), sem("a_var"), sem("a_veps"), sem("a_rstd"), sem("a_xn")
        a_tr, a_xnT, a_rvk, a_evac = sem("a_tr"), sem("a_xnT"), sem("a_rvk"), sem("a_evac")
        a_carry, a_o, a_z, a_dd, a_kko = sem("a_carry"), sem("a_o"), sem("a_z"), sem("a_dd"), sem("a_kko")
        a_eo, a_ek, a_kv, a_relu, a_mix, a_pq = sem("a_eo"), sem("a_ek"), sem("a_kv"), sem("a_relu"), sem("a_mix"), sem("a_pq")
        a_bv, a_old, a_oldp, a_num, a_den, a_nsig = sem("a_bv"), sem("a_old"), sem("a_oldp"), sem("a_num"), sem("a_den"), sem("a_nsig")
        a_ln, a_r0, a_nt, a_rec, a_y = sem("a_ln"), sem("a_r0"), sem("a_nt"), sem("a_rec"), sem("a_y")
        a_out, a_resid = sem("a_out"), sem("a_resid")
        setup_step = sem("setup_step")

        with ExitStack() as pa:
            wr = buf(pa, "wr", [KH, 3 * H])
            wo1 = buf(pa, "wo1", [KH, H])
            dec = buf(pa, "dec", [KH])
            fst = buf(pa, "fst", [KH])
            nfst = buf(pa, "nfst", [KH])
            lutS = buf(pa, "lutS", [16])
            lutX = buf(pa, "lutX", [8], I32)
            X = [buf(pa, f"X{s}", [TT, H]) for s in range(2)]
            XR = buf(pa, "XR", [TT, H])
            xn = buf(pa, "xn", [TT, H])
            xnT = buf(pa, "xnT", [KH, CH])
            sg = [buf(pa, f"sg{s}", [KH, CH]) for s in range(2)]
            vv = [buf(pa, f"vv{s}", [KH, CH]) for s in range(2)]
            kk = [buf(pa, f"kk{s}", [KH, CH]) for s in range(2)]
            oX = buf(pa, "oX", [KH, CH + 1])
            pX = buf(pa, "pX", [KH, CH + 1])
            qX = buf(pa, "qX", [KH, CH + 1])
            EO = buf(pa, "EO", [KH, CH])
            EK = buf(pa, "EK", [KH, CH])
            Z = buf(pa, "Z", [KH, CH])
            M = buf(pa, "M", [KH, CH])
            MA = buf(pa, "MA", [KH, CH])
            MB = buf(pa, "MB", [KH, CH])
            yT = buf(pa, "yT", [KH, CH])
            ix = [buf(pa, f"ix{s}", [DEC], I32) for s in range(2)]
            bit = [buf(pa, f"bit{b}", [DEC], I32) for b in range(4)]
            nA = [buf(pa, f"nA{s}", [DEC], I32) for s in range(2)]
            nB, nC, nE = (buf(pa, f"n{c}", [DEC], I32) for c in "BCE")
            trP = pa.enter_context(nc.psum_tensor("trP", [P, KH, CH], F32))
            rvkP = [pa.enter_context(nc.psum_tensor(f"rvkP{s}", [P, KH, CH], F32)) for s in range(2)]
            outP = pa.enter_context(nc.psum_tensor("outP", [P, TT, H], F32))
            block = pa.enter_context(nc.Block())

            def steps_a(step, eng):
                step(-1, 1, True, False)
                step(0, 0, True, True)
                step(1, 1, True, True)
                with eng.Fori(2, NC - 3, 2) as c:
                    step(c, 0, True, True)
                    step(c + 1, 1, True, True)
                step(NC - 2, 0, True, True)
                step(NC - 1, 1, False, True)

            @block.sync
            def _(sp):
                sp.dma_start(X[0][:], x_t[0]).then_inc(x_loaded[0], 16)
                sp.dma_start(wr[:], w_rvk.rearrange("(k p) n -> p k n", p=P)).then_inc(par_loaded, 16)
                sp.dma_start(dec[:], decay).then_inc(par_loaded, 16)
                sp.dma_start(fst[:], first).then_inc(par_loaded, 16)
                sp.dma_start(lutS[:], lut.partition_broadcast(P)).then_inc(par_loaded, 16)
                sp.dma_start(wo1[:], w_out.rearrange("(k p) n -> p k n", p=P)).then_inc(par_loaded, 16)
                sp.dma_start(X[1][:], x_t[1]).then_inc(x_loaded[1], 16)
                for q in range(2):
                    sp.dma_start(ix[q][:], idx[:, q * DEC:(q + 1) * DEC]).then_inc(idx_loaded[q], 16)

                def store_piece(c, more):
                    for h in range(2):
                        q = 2 * c + h
                        sp.wait_ge(dec_ready, q + 1)
                        sp.wait_ge(par_loaded, 80)
                        sp.dma_start(wffn[:, bass.ds(q * DEC, DEC)], nA[h][:].bitcast(F32)).then_inc(dec_stored[h], 16)
                        if more:
                            sp.dma_start(ix[h][:], idx[:, bass.ds((q + 2) * DEC, DEC)]).then_inc(idx_loaded[h], 16)

                def step(c, s, more_x, more_d, more_idx):
                    if more_x:
                        sp.wait_ge(a_xn, TT * (c + 2))
                        sp.wait_ge(par_loaded, 80)
                        sp.dma_start(X[1 - s][:], x_t[c + 3]).then_inc(x_loaded[1 - s], 16)
                    sp.wait_ge(x1_stored, 16 * c)
                    sp.wait_ge(par_loaded, 80)
                    sp.dma_start(XR[:], x_t[c]).then_inc(xr_loaded, 16)
                    if more_d:
                        store_piece(c + 1, more_idx)
                    sp.wait_ge(a_resid, c + 1)
                    sp.wait_ge(par_loaded, 80)
                    sp.dma_start(x1_d[c], XR[:]).then_inc(x1_stored, 16)

                sp.wait_ge(a_xn, TT)
                sp.dma_start(X[0][:], x_t[2]).then_inc(x_loaded[0], 16)
                store_piece(0, True)
                step(0, 0, True, True, True)
                step(1, 1, True, True, True)
                with sp.Fori(2, NC - 5, 2) as c:
                    step(c, 0, True, True, True)
                    step(c + 1, 1, True, True, True)
                step(NC - 4, 0, True, True, True)
                step(NC - 3, 1, False, True, True)
                step(NC - 2, 0, False, True, False)
                step(NC - 1, 1, False, False, False)
                sp.wait_ge(x1_stored, 16 * NC)
                for h in range(2):
                    sp.wait_ge(dec_stored[h], 16 * NC)

            @block.gpsimd
            def _(pool):
                nc.gpsimd.memset(ident[:], 0.0).then_inc(ident_zero, 1)
                nc.gpsimd.memset(mhalf[:], -0.5).then_inc(const_ready, 1)
                pool.wait_ge(ident_zero, 1)
                nc.gpsimd.affine_select(out=ident[:], in_=ident[:], compare_op=ALU.not_equal, fill=1.0, base=0,
                                        pattern=[[-1, P]], channel_multiplier=1).then_inc(const_ready, 1)
                pool.wait_ge(const_ready, 2)

                def root(g):
                    pool.wait_ge(a_veps, g + 1)
                    nc.gpsimd.tensor_tensor(rstd[:], veps[:], mhalf[:], ALU.pow).then_inc(a_rstd, 1)

                def step(c, s, front, back):
                    if not back:
                        root(0)
                        root(1)
                    if back:
                        pool.wait_ge(a_o, KH * (c + 1))
                        pool.wait_ge(a_pq, 2 * KH * c)
                        nc.gpsimd.tensor_tensor(EO[:], oX[:, :, 0:CH], oX[:, :, 1:CH + 1], ALU.subtract).then_inc(a_dd, 1)
                        nc.gpsimd.tensor_tensor(EK[:], kk[s][:], oX[:, :, 1:CH + 1], ALU.subtract).then_inc(a_kko, 1)
                        pool.wait_ge(a_y, c)
                        nc.gpsimd.tensor_tensor(Z[:], kk[s][:], oX[:, :, 0:CH], ALU.subtract).then_inc(a_z, 1)
                        pool.wait_ge(a_ek, c + 1)
                        pool.wait_ge(a_evac, 3 * (c + 1))
                        pool.wait_ge(a_nt, c)
                        nc.gpsimd.tensor_tensor(M[:], EK[:], vv[s][:], ALU.mult).then_inc(a_kv, 1)
                        pool.wait_ge(a_mix, c + 1)
                        pool.wait_ge(a_kv, c + 1)
                        nc.gpsimd.tensor_tensor(vv[s][:], MB[:], vv[s][:], ALU.mult).then_inc(a_bv, 1)
                        pool.wait_ge(a_pq, 2 * KH * (c + 1))
                        nc.gpsimd.tensor_tensor(Z[:], MA[:], pX[:, :, 0:CH], ALU.mult).then_inc(a_oldp, 1)
                        pool.wait_ge(a_oldp, c + 1)
                        nc.gpsimd.tensor_tensor(Z[:], Z[:], vv[s][:], ALU.add).then_inc(a_num, 1)
                        pool.wait_ge(a_num, c + 1)
                        nc.gpsimd.tensor_tensor(Z[:], Z[:], sg[s][:], ALU.mult).then_inc(a_nsig, 1)
                        if front and not (isinstance(c, int) and c == NC - 2):
                            root(c + 2)
                        pool.wait_ge(a_r0, c + 1)
                        nc.gpsimd.tensor_tensor(MB[:], M[:], MA[:], ALU.mult).then_inc(a_nt, 1)
                        pool.wait_ge(a_rec, c + 1)
                        pool.wait_ge(a_out, c)
                        nc.gpsimd.tensor_tensor(yT[:], Z[:], MB[:], ALU.mult).then_inc(a_y, 1)

                steps_a(step, pool)

            @block.scalar
            def _(act):
                act.wait_ge(par_loaded, 80)
                nc.scalar.activation(dec[:], dec[:], ACT.Exp).then_inc(setup_step, 1)

                def step(c, s, front, back):
                    f, sf = c + 1, 1 - s
                    if front:
                        act.wait_ge(a_tr, f + 1)
                        act.wait_ge(a_rvk, 3 * f)
                        nc.scalar.activation(xnT[:], trP[:], ACT.Copy).then_inc(a_xnT, 1)
                    if back:
                        nc.scalar.preload_act_table_set("natural_log_exp_and_others")
                        act.wait_ge(a_dd, c + 1)
                        act.wait_ge(setup_step, 4)
                        for m in range(KH):
                            nc.scalar.activation(EO[:, m, :], EO[:, m, :], ACT.Exp, bias=dec[:, m:m + 1]).then_inc(a_eo, 1)
                        act.wait_ge(a_kko, c + 1)
                        nc.scalar.activation(EK[:], EK[:], ACT.Exp).then_inc(a_ek, 1)
                    if back:
                        act.wait_ge(a_z, c + 1)
                        act.wait_ge(a_y, c)
                        for m in range(KH):
                            nc.scalar.activation(MA[:, m, :], Z[:, m, :], ACT.Relu, bias=fst[:, m:m + 1]).then_inc(a_relu, 1)
                        for m in range(KH):
                            nc.scalar.activation(MB[:, m, :], Z[:, m, :], ACT.Relu, bias=nfst[:, m:m + 1], scale=-1.0).then_inc(a_relu, 1)
                        act.wait_ge(a_relu, 2 * KH * (c + 1))
                        nc.scalar.activation(MA[:], MA[:], ACT.Exp, scale=-1.0)
                        nc.scalar.activation(MB[:], MB[:], ACT.Exp, scale=-1.0).then_inc(a_mix, 1)
                    if front:
                        act.wait_ge(a_rvk, 3 * f + 1)
                        act.wait_ge(a_z, least(f - 1))
                        act.wait_ge(a_kko, least(f - 1))
                        nc.scalar.activation(kk[sf][:], rvkP[sf][:], ACT.Copy).then_inc(a_evac, 1)
                    if back:
                        act.wait_ge(a_den, c + 1)
                        act.wait_ge(a_oldp, c + 1)
                        nc.scalar.activation(MA[:], M[:], ACT.Ln).then_inc(a_ln, 1)
                        act.wait_ge(a_ln, c + 1)
                        nc.scalar.activation(MA[:], MA[:], ACT.Exp, scale=-1.0).then_inc(a_r0, 1)
                    if front:
                        act.wait_ge(a_rvk, 3 * f + 2)
                        act.wait_ge(a_nsig, least(f - 1))
                        nc.scalar.activation(sg[sf][:], rvkP[1 - sf][:], ACT.Sigmoid).then_inc(a_evac, 1)
                        act.wait_ge(a_rvk, 3 * f + 3)
                        act.wait_ge(a_num, least(f - 1))
                        nc.scalar.activation(vv[sf][:], rvkP[sf][:], ACT.Copy).then_inc(a_evac, 1)

                steps_a(step, act)

            @block.tensor
            def _(pe):
                pe.wait_ge(const_ready, 2)
                pe.wait_ge(par_loaded, 80)

                def product(c):
                    pe.wait_ge(a_y, c + 1)
                    pe.wait_ge(a_resid, c)
                    for t in range(TT):
                        for k in range(KH):
                            last = nc.tensor.matmul(outP[:, t, :], yT[:, k, t * P:(t + 1) * P], wo1[:, k, :],
                                                    start=(k == 0), stop=(k == KH - 1))
                    last.then_inc(a_out, 1)

                def step(c, s, front, back):
                    f, sf = c + 1, 1 - s
                    if front:
                        pe.wait_ge(a_xn, TT * (f + 1))
                        pe.wait_ge(a_xnT, f)
                        for k in range(KH):
                            for t in range(TT):
                                last = nc.tensor.transpose(trP[:, k, t * P:(t + 1) * P], xn[:, t, k * P:(k + 1) * P], ident[:])
                        last.then_inc(a_tr, 1)
                    if back and not (isinstance(c, int) and c == 0):
                        product(c - 1)
                    if front:
                        pe.wait_ge(a_xnT, f + 1)
                        for g, part in enumerate((2, 0, 1)):
                            pe.wait_ge(a_evac, least(3 * f + g - 1))
                            for m in range(KH):
                                for k in range(KH):
                                    last = nc.tensor.matmul(rvkP[(sf + g) % 2][:, m, :], wr[:, k, part * H + m * P:part * H + (m + 1) * P],
                                                            xnT[:, k, :], start=(k == 0), stop=(k == KH - 1))
                            last.then_inc(a_rvk, 1)
                steps_a(step, pe)
                product(NC - 1)

            @block.vector
            def _(dve):
                V = nc.vector
                V.memset(keep[:], 1.0)
                V.memset(floor[:], 0.0)
                for t in (oX, pX, qX):
                    V.memset(t[:, :, CH:CH + 1], 0.0)
                V.memset(veps[:], 1.0).then_inc(setup_step, 1)
                dve.wait_ge(setup_step, 2)
                V.memset(keep[:, 0:NC:SEQ], 0.0)
                V.memset(floor[:, 0:NC:SEQ], FLOOR)
                V.tensor_scalar(dec[:], dec[:], -1.0, None, ALU.mult).then_inc(setup_step, 1)
                lutI = lutS[:].bitcast(I32).rearrange("p (a b) -> p a b", b=2)
                V.tensor_tensor(lutX[:], lutI[:, :, 0], lutI[:, :, 1], ALU.bitwise_xor)
                V.tensor_scalar(nfst[:], fst[:], -1.0, None, ALU.mult).then_inc(setup_step, 1)
                dve.wait_ge(setup_step, 4)

                def alone(semaphore, count):
                    dve.wait_ge(semaphore, count)
                    V.memset(tick[:], 0.0)

                def decode(c, h):
                    q, a = 2 * c + h, nA[h]

                    def leaf(dst, j, k=0):
                        if k:
                            dve.wait_ge(dec_step, 18 * q + k)
                        return V.tensor_scalar(dst[:], bit[0][:], lutX[:, j:j + 1], lutI[:, j, 0:1], ALU.bitwise_and, ALU.bitwise_xor)

                    def pick(dst, b, src, k=0):
                        if k:
                            alone(dec_step, 18 * q + k)
                        return V.copy_predicated(dst[:], bit[b][:], src[:])

                    dve.wait_ge(idx_loaded[h], 16 * (c + 1))
                    dve.wait_ge(dec_ready, q)
                    V.tensor_scalar(bit[0][:], ix[h][:], 31, 31, ALU.logical_shift_left, ALU.arith_shift_right).then_inc(dec_step, 1)
                    for b in range(1, 4):
                        V.tensor_scalar(bit[b][:], ix[h][:], 1 << b, None, ALU.bitwise_and).then_inc(dec_step, 1)
                    dve.wait_ge(dec_stored[h], 16 * c)
                    dve.wait_ge(dec_step, 18 * q + 1)
                    leaf(a, 0).then_inc(dec_step, 1)
                    leaf(nB, 1).then_inc(dec_step, 1)
                    leaf(nC, 2, 6).then_inc(dec_step, 1)
                    pick(a, 1, nB).then_inc(dec_step, 1)
                    leaf(nB, 3, 8).then_inc(dec_step, 1)
                    leaf(nE, 4, 9).then_inc(dec_step, 1)
                    pick(nC, 1, nB).then_inc(dec_step, 1)
                    leaf(nB, 5, 11).then_inc(dec_step, 1)
                    pick(a, 2, nC).then_inc(dec_step, 1)
                    leaf(nC, 6, 13).then_inc(dec_step, 1)
                    pick(nE, 1, nB).then_inc(dec_step, 1)
                    leaf(nB, 7, 15).then_inc(dec_step, 1)
                    pick(nC, 1, nB, 16).then_inc(dec_step, 1)
                    pick(nE, 2, nC, 17).then_inc(dec_step, 1)
                    pick(a, 3, nE, 18).then_inc(dec_ready, 1)

                def resid(c):
                    dve.wait_ge(a_out, c + 1)
                    dve.wait_ge(xr_loaded, 16 * (c + 1))
                    V.tensor_tensor(XR[:], outP[:], XR[:], ALU.add).then_inc(a_resid, 1)

                def stats(g, s):
                    dve.wait_ge(x_loaded[s], 8 * (g - s) + 16)
                    dve.wait_ge(a_xn, TT * g)
                    for t in range(TT):
                        V.bn_stats(bnst[:, t, :], X[s][:, t, :]).then_inc(a_stat, 1)
                    alone(a_stat, TT * (g + 1))
                    for t in range(TT):
                        V.bn_aggr(mv[:, t, :], bnst[:, t, :]).then_inc(a_var, 1)
                    dve.wait_ge(a_var, TT * (g + 1))
                    V.tensor_scalar(veps[:], mv[:, :, 1], EPS, None, ALU.add).then_inc(a_veps, 1)

                def norm(g, s):
                    dve.wait_ge(a_rstd, g + 1)
                    dve.wait_ge(a_tr, g)
                    for t in range(TT):
                        V.tensor_scalar(xn[:, t, :], X[s][:, t, :], mv[:, t, 0:1], rstd[:, t:t + 1],
                                        ALU.subtract, ALU.mult).then_inc(a_xn, 1)

                def step(c, s, front, back):
                    f, sf = c + 1, 1 - s
                    if not back:
                        stats(0, 0)
                        norm(0, 0)
                        stats(1, 1)
                        decode(0, 0)
                        decode(0, 1)
                        norm(1, 1)
                    if back:
                        dve.wait_ge(a_dd, c)
                        dve.wait_ge(a_oldp, c)
                        dve.wait_ge(a_old, c)
                        V.tensor_scalar(oX[:, :, 0:1], oX[:, :, CH:CH + 1], keep[:, bass.ds(c, 1)], floor[:, bass.ds(c, 1)],
                                        ALU.mult, ALU.add).then_inc(a_carry, 1)
                        V.tensor_scalar(pX[:, :, 0:1], pX[:, :, CH:CH + 1], keep[:, bass.ds(c, 1)], None, ALU.mult).then_inc(a_carry, 1)
                        V.tensor_scalar(qX[:, :, 0:1], qX[:, :, CH:CH + 1], keep[:, bass.ds(c, 1)], None, ALU.mult).then_inc(a_carry, 1)
                        dve.wait_ge(a_evac, 3 * c + 1)
                        dve.wait_ge(a_carry, 3 * (c + 1))
                        for m in range(KH):
                            V.tensor_tensor_scan(oX[:, m, 1:CH + 1], dec[:, m:m + 1].to_broadcast([P, CH]), kk[s][:, m, :],
                                                 oX[:, m, 0:1], ALU.add, ALU.max).then_inc(a_o, 1)
                        if front:
                            decode(c + 1, 0)
                        dve.wait_ge(a_eo, KH * (c + 1))
                        dve.wait_ge(a_kv, c + 1)
                        for m in range(KH):
                            V.tensor_tensor_scan(pX[:, m, 1:CH + 1], EO[:, m, :], M[:, m, :], pX[:, m, 0:1], ALU.mult, ALU.add).then_inc(a_pq, 1)
                            V.tensor_tensor_scan(qX[:, m, 1:CH + 1], EO[:, m, :], EK[:, m, :], qX[:, m, 0:1], ALU.mult, ALU.add).then_inc(a_pq, 1)
                        dve.wait_ge(a_mix, c + 1)
                        dve.wait_ge(a_pq, 2 * KH * (c + 1))
                        V.tensor_tensor(M[:], MA[:], qX[:, :, 0:CH], ALU.mult).then_inc(a_old, 1)
                        dve.wait_ge(a_old, c + 1)
                        V.tensor_tensor(M[:], M[:], MB[:], ALU.add).then_inc(a_den, 1)
                        if not (isinstance(c, int) and c == 0):
                            resid(c - 1)
                        more = front and not (isinstance(c, int) and c == NC - 2)
                        if more:
                            stats(c + 2, s)
                        if front:
                            decode(c + 1, 1)
                        if more:
                            norm(c + 2, s)
                        dve.wait_ge(a_nt, c + 1)
                        V.scalar_tensor_tensor(MB[:], MB[:], 2.0, MA[:], ALU.subtract, ALU.mult, reverse0=True).then_inc(a_rec, 1)

                steps_a(step, dve)
                resid(NC - 1)

        win = buf(ctx, "win", [KH, 2 * E])
        wx = buf(ctx, "wx", [ME, R + 2 * S])
        wdt = buf(ctx, "wdt", [E])
        wo = buf(ctx, "wo", [ME, H])
        cw = buf(ctx, "cw", [ME, KC])
        cb = buf(ctx, "cb", [ME])
        bdt = buf(ctx, "bdt", [ME])
        dsk = buf(ctx, "dsk", [ME])
        A = buf(ctx, "A", [ME, S])
        XM = buf(ctx, "XM", [TT, H])
        X3 = buf(ctx, "X3", [TT, H])
        nrm = buf(ctx, "nrm", [TT, H])
        nT = buf(ctx, "nT", [KH, CH])
        hT = buf(ctx, "hT", [MI, CH])
        U = buf(ctx, "U", [ME, CH])
        delta = buf(ctx, "delta", [ME, CH])
        yacc = buf(ctx, "yacc", [ME, CH])
        sgm = buf(ctx, "sgm", [ME, CH])
        bcS = buf(ctx, "bcS", [CH])
        dtl = buf(ctx, "dtl", [CH])
        xext = [buf(ctx, f"xext{s}", [2, CH + KC - 1]) for s in range(2)]
        cc = buf(ctx, "cc", [ME, KC - 1])
        hc = buf(ctx, "hc", [S, ME])
        BC = [buf(ctx, f"BC{s}", [2, CH]) for s in range(3)]
        dBu = [buf(ctx, f"dBu{s}", [2, CH]) for s in range(4)]
        prod = [buf(ctx, f"prod{s}", [2, CH]) for s in range(2)]
        W = [ctx.enter_context(nc.psum_tensor(f"W{s}", [P, 4, CH], F32)) for s in range(2)]
        D = ctx.enter_context(nc.psum_tensor("D", [P, ME, CH], F32))

        wts_loaded, small_loaded = sem("wts_loaded"), sem("small_loaded")
        b_setup = sem("b_setup")
        xm_loaded, x2_stored, x3_loaded, out_stored = sem("xm_loaded"), sem("x2_stored"), sem("x3_loaded"), sem("out_stored")
        bc_stored = sem("bc_stored")
        bc_loaded = [sem(f"bc_loaded{s}") for s in range(3)]
        n_stat, n_var, n_veps, n_rstd, n_done = sem("n_stat"), sem("n_var"), sem("n_veps"), sem("n_rstd"), sem("n_done")
        n_tr, n_T = sem("n_tr"), sem("n_T")
        f_gu, f_silu, f_h, f_out, f_res = sem("f_gu"), sem("f_silu"), sem("f_h"), sem("f_out"), sem("f_res")
        m_x, m_ext, m_tap, m_in, m_conv, m_cc = sem("m_x"), sem("m_ext"), sem("m_tap"), sem("m_in"), sem("m_conv"), sem("m_cc")
        m_u, m_skip, m_g, m_sg, m_bc, m_bcS = sem("m_u"), sem("m_skip"), sem("m_g"), sem("m_sg"), sem("m_bc"), sem("m_bcS")
        m_dt, m_dtl, m_dp, m_abs, m_relu = sem("m_dt"), sem("m_dtl"), sem("m_dp"), sem("m_abs"), sem("m_relu")
        m_exp, m_ln, m_delta, m_du = sem("m_exp"), sem("m_ln"), sem("m_delta"), sem("m_du")
        s_dA, s_dBu, s_scan, s_hc = sem("s_dA"), sem("s_dBu"), sem("s_scan"), sem("s_hc")
        s_prod, s_hC, s_acc = sem("s_prod"), sem("s_hC"), sem("s_acc")
        m_y, m_out, m_res = sem("m_y"), sem("m_out"), sem("m_res")

        def early(i):
            return ("F1", 1) if isinstance(i, int) and i == 0 else ("F1", i + 2)

        def late(i):
            return ("F1", 2) if isinstance(i, int) and i == 0 else ("F2", i - 1)

        norms, ffns, loads = [("F1", 0), ("M", 0)], [("F1", 0)], [("x1", 0)]
        for i in range(NC):
            norms += [early(i)] * (i + 2 < NC) + [late(i)] + [("M", i + 1)] * (i + 1 < NC)
            ffns += [early(i)] * (i + 2 < NC) + [late(i)]
            loads += [("x1", i + 2)] * (i + 2 < NC) + [("x2", i + 1)] * (0 < i < NC - 1)
        norms, ffns = norms + [("F2", NC - 1)], ffns + [("F2", NC - 1)]

        def number(order, kind, chunk):
            if isinstance(chunk, int):
                return order.index((kind, chunk))
            lo = {"F1": 3, "F2": 0, "M": 2, "x1": 3, "x2": 2}[kind]
            at = [order.index((kind, n)) for n in range(lo, lo + NC - 3)]
            step = at[1] - at[0]
            assert at == list(range(at[0], at[-1] + 1, step))
            return chunk * step + (at[0] - lo * step)

        norm_no = lambda kind, chunk: number(norms, kind, chunk)
        ffn_no = lambda kind, chunk: number(ffns, kind, chunk)
        load_no = lambda kind, chunk: number(loads, kind, chunk)

        def steps_b(step, eng):
            step(0, False, True, True)
            with eng.Fori(1, NC - 2) as i:
                step(i, True, True, True)
            step(NC - 2, True, False, True)
            step(NC - 1, True, False, False)

        def places(f1):
            if f1:
                return dict(norm=F2_NORM, evac=F2_EVAC, silu=F2_SILU, res=F2_RES, m_stat=M_STAT, m_norm=M_NORM, m_evac=NE)
            return dict(norm=F2_STAT + 1, evac=F1_EVAC + 2, silu=[e + 3 for e in F1_SILU], res=F1_RES + 3,
                        m_stat=F1_RES - 6, m_norm=F1_RES - 4, m_evac=F1_RES + 7)

        SIDE_0, SIDE_EARLY, SIDE_LAST = 1, 0, 0

        def side_late(f1):
            return 1 - SIDE_EARLY if f1 else SIDE_EARLY

        def pool_pairs(f1):
            return 3 if f1 else 2

        def steps_less(i):
            return max(i - (NC - 2), 0) if isinstance(i, int) else 0

        def pool_sums(i):
            return S * (3 * i - steps_less(i))

        def dve_sums(i):
            return S * (i + steps_less(i))

        def rows(p):
            return [(m, LAST if m == MI - 1 else P) for m in (2 * p, 2 * p + 1) if m < MI]

        with nc.Block() as block:
            @block.sync
            def _(sp):
                sp.dma_start(XM[:], x1_d[0]).then_inc(xm_loaded, 16)
                for t, d in ((A, a_log), (cw, conv_w), (cb, conv_b), (bdt, b_dt), (dsk, d_skip)):
                    sp.dma_start(t[:], d).then_inc(small_loaded, 16)
                sp.dma_start(X3[:], x1_d[1]).then_inc(x3_loaded, 16)
                sp.dma_start(win[:], w_in.rearrange("(k p) n -> p k n", p=P)).then_inc(wts_loaded, 16)
                sp.dma_start(wx[:], w_x.rearrange("(k p) n -> p k n", p=P)).then_inc(wts_loaded, 16)
                sp.dma_start(wdt[:], w_dt).then_inc(wts_loaded, 16)
                sp.dma_start(wo[:], w_o.rearrange("(k p) n -> p k n", p=P)).then_inc(wts_loaded, 16)
                def keep_x2(i, rows_):
                    sp.wait_ge(f_res, ffn_no("F1", i) + 1)
                    sp.wait_ge(small_loaded, 80)
                    sp.dma_start(x2_d[i], rows_[:]).then_inc(x2_stored, 16)

                def load_x2(i, stored):
                    sp.wait_ge(x2_stored, 16 * stored)
                    sp.wait_ge(small_loaded, 80)
                    sp.dma_start(XM[:], x2_d[i]).then_inc(xm_loaded, 16)

                def step(i, back, f1, more):
                    if f1:
                        sp.wait_ge(n_done, TT * (norm_no("M", i) + 1))
                        sp.wait_ge(small_loaded, 80)
                        sp.dma_start(XM[:], x1_d[i + 2]).then_inc(xm_loaded, 16)
                    elif more:
                        sp.wait_ge(n_done, TT * (norm_no("M", i) + 1))
                        load_x2(i + 1, NC)
                    sp.wait_ge(m_bcS, i + 1)
                    sp.wait_ge(small_loaded, 80)
                    sp.dma_start(bc_d[i].rearrange("a n t -> (a n) t"), bcS[0:2 * S, :]).then_inc(bc_stored, 16)
                    sp.wait_ge(bc_stored, 16 * (i + 1))
                    sp.wait_ge(small_loaded, 80)
                    for n in range(S):
                        if n >= 3:
                            sp.wait_ge(s_prod, NE * i + 4 * (n - 2))
                            sp.wait_ge(small_loaded, 80)
                        sp.dma_start(BC[n % 3][:], bc_d[i][:, n, :].partition_broadcast(P)).then_inc(bc_loaded[n % 3], 16)
                        if n == 10 and f1:
                            if back:
                                keep_x2(i + 2, XM)
                            else:
                                keep_x2(1, X3)
                        if n == 12 and f1 and back:
                            load_x2(i + 1, i + 3)
                    if not back:
                        keep_x2(2, XM)
                        sp.wait_ge(n_done, TT * (norm_no("M", 1) + 1))
                        sp.wait_ge(x2_stored, 16 * 3)
                    if back:
                        sp.wait_ge(f_res, ffn_no("F2", i - 1) + 1)
                        sp.wait_ge(small_loaded, 80)
                        sp.dma_start(out_t[i - 1], X3[:]).then_inc(out_stored, 16)
                        sp.wait_ge(out_stored, 16 * i)
                        sp.wait_ge(small_loaded, 80)
                    sp.dma_start(X3[:], x2_d[i]).then_inc(x3_loaded, 16)

                keep_x2(0, XM)
                sp.wait_ge(x2_stored, 16)
                steps_b(step, sp)
                sp.wait_ge(f_res, ffn_no("F2", NC - 1) + 1)
                sp.dma_start(out_t[NC - 1], X3[:]).then_inc(out_stored, 16)
                sp.wait_ge(out_stored, 16 * NC)

            @block.gpsimd
            def _(pool):
                def root(L):
                    pool.wait_ge(n_veps, L + 1)
                    pool.wait_ge(n_done, TT * L)
                    nc.gpsimd.tensor_tensor(rstd[:], veps[:], mhalf[:], ALU.pow).then_inc(n_rstd, 1)

                def step(i, back, f1, more):
                    at = places(f1)
                    if f1:
                        root(norm_no(*early(i)))

                    def outer(e):
                        n, j = divmod(e, 4)
                        slot = n % 3
                        if j == 0:
                            pool.wait_ge(bc_loaded[slot], 16 * ((6 if slot == 0 else 5) * i + n // 3 + 1))
                        if e < 4:
                            pool.wait_ge(m_du, 4 * i + e + 1)
                        else:
                            pool.wait_ge(s_scan, 2 * NE * i + 2 * (e - 3))
                        nc.gpsimd.tensor_tensor(dBu[e % 4][:], U[:, 2 * j:2 * j + 2, :], BC[slot][:, 0:1, :].to_broadcast([P, 2, CH]),
                                                ALU.mult).then_inc(s_dBu, 1)

                    def add(e):
                        n, j = divmod(e, 4)
                        r = pool_pairs(f1) * n + j
                        pool.wait_ge(s_prod, NE * i + e + 1)
                        if r == 0:
                            pool.wait_ge(m_skip, ME * (i + 1))
                        if n:
                            pool.wait_ge(s_acc, pool_sums(i) + r - pool_pairs(f1) + 1)
                        y = yacc[:, 2 * j:2 * j + 2, :]
                        nc.gpsimd.tensor_tensor(y, y, prod[r % 2][:], ALU.add).then_inc(s_acc, 1)

                    for e in range(4):
                        outer(e)
                    for e in range(NE):
                        if e + 4 < NE:
                            outer(e + 4)
                        if e % 4 < pool_pairs(f1):
                            add(e)
                        if e == F2_STAT:
                            root(norm_no(*late(i)))
                        if more and e == at["m_stat"]:
                            root(norm_no("M", i + 1))

                for L in range(2):
                    root(L)
                steps_b(step, pool)
                root(norm_no("F2", NC - 1))

            @block.scalar
            def _(act):
                N_ = nc.scalar

                def evac(L, side):
                    act.wait_ge(n_tr, L + 1)
                    N_.activation(nT[:], W[side][:], ACT.Copy).then_inc(n_T, 1)

                def silu(F, L, p, side):
                    act.wait_ge(f_gu, NP * F + p + 1)
                    if p < 2:
                        act.wait_ge(n_tr, L + 1)
                    else:
                        act.wait_ge(f_h, NP * F + p - 1)
                    r = rows(p)
                    w = len(r) * CH
                    N_.activation(nrm[0:r[0][1], p % 2, 0:w], W[(side + p) % 2][0:r[0][1], 0:len(r), :].rearrange("p a t -> p (a t)"),
                                  ACT.Silu).then_inc(f_silu, 1)

                def step(i, back, f1, more):
                    for q in range(ME // 2):
                        act.wait_ge(m_x, 2 * i + q // 2 + 1)
                        act.wait_ge(m_cc, 4 * i + max(q - 1, 0))
                        act.wait_ge(m_conv, 24 * i + 6 * max(q - 1, 0))
                        src = W[q // 2]
                        a = 2 * (q % 2)
                        N_.activation(xext[q % 2][:, :, KC - 1:], src[:, a:a + 2, :], ACT.Copy).then_inc(m_ext, 1)
                        act.wait_ge(s_dBu, NE * i)
                        for h in range(2):
                            m = 2 * q + h
                            N_.activation(U[:, m, :], src[:, a + h, :], ACT.Identity, bias=cb[:, m:m + 1],
                                          scale=cw[:, m, KC - 1:KC]).then_inc(m_tap, 1)
                        for z in (q - 1, q) if q % 2 else ():
                            act.wait_ge(m_conv, 24 * i + 6 * (z + 1))
                            N_.activation(U[:, 2 * z:2 * z + 2, :], U[:, 2 * z:2 * z + 2, :], ACT.Silu).then_inc(m_u, 1)
                    act.wait_ge(m_dt, i + 1)
                    N_.activation(dtl[:], W[0][:, 0, :], ACT.Copy).then_inc(m_dtl, 1)
                    act.wait_ge(m_bc, i + 1)
                    act.wait_ge(bc_stored, 16 * i)
                    N_.activation(bcS[0:2 * S, :], W[0][0:2 * S, 2, :], ACT.Copy).then_inc(m_bcS, 1)
                    N_.preload_act_table_set("natural_log_exp_and_others")
                    act.wait_ge(m_u, 4 * (i + 1))
                    act.wait_ge(m_y, 2 * i)
                    for m in range(ME):
                        N_.activation(yacc[:, m, :], U[:, m, :], ACT.Identity, scale=dsk[:, m:m + 1]).then_inc(m_skip, 1)
                    act.wait_ge(s_scan, 2 * NE * i)
                    at = places(f1)
                    for k in range(ME // 2 + 2):
                        if k < 4:
                            act.wait_ge(m_dp, 4 * i + k + 1)
                            for h in range(2):
                                m = 2 * k + h
                                N_.activation(dBu[k][:, h, :], D[:, m, :], ACT.Abs, bias=bdt[:, m:m + 1]).then_inc(m_abs, 1)
                        if 1 <= k < 5:
                            act.wait_ge(m_abs, ME * i + 2 * k)
                            N_.activation(dBu[k - 1][:], dBu[k - 1][:], ACT.Exp, scale=-1.0).then_inc(m_exp, 1)
                        if k >= 2:
                            act.wait_ge(m_exp, 4 * i + k - 1)
                            N_.activation(dBu[k - 2][:], dBu[k - 2][:], ACT.Ln, bias=1.0).then_inc(m_ln, 1)
                    for e in range(NE):
                        n, j = divmod(e, 4)
                        if e >= 4:
                            act.wait_ge(s_prod, NE * i + e - 3)
                        else:
                            act.wait_ge(m_delta, 4 * i + e + 1)
                        for m in (2 * j, 2 * j + 1):
                            N_.activation(D[:, m, :], delta[:, m, :], ACT.Exp, scale=A[:, m, n:n + 1]).then_inc(s_dA, 1)
                        for h in range(2):
                            if e == G_SILU[h]:
                                act.wait_ge(m_g, 2 * i + h + 1)
                                act.wait_ge(m_out, TT * i)
                                N_.activation(sgm[:, 4 * h:4 * h + 4, :], W[h][:], ACT.Silu).then_inc(m_sg, 1)
                        if f1 and e == F1_EVAC:
                            evac(norm_no(*early(i)), SIDE_EARLY)
                        if e == at["evac"]:
                            evac(norm_no(*late(i)), side_late(f1))
                        for p in range(NP):
                            if f1 and e == F1_SILU[p]:
                                silu(ffn_no(*early(i)), norm_no(*early(i)), p, SIDE_EARLY)
                            if e == at["silu"][p]:
                                silu(ffn_no(*late(i)), norm_no(*late(i)), p, side_late(f1))
                        if more and e == min(at["m_evac"], NE - 1):
                            evac(norm_no("M", i + 1), 1 - side_late(f1))

                act.wait_ge(small_loaded, 80)
                N_.activation(A[:], A[:], ACT.Exp).then_inc(b_setup, 1)
                evac(0, SIDE_0)
                for p in range(NP):
                    silu(0, 0, p, SIDE_0)
                evac(1, 1 - SIDE_0)
                act.wait_ge(b_setup, 3)
                steps_b(step, act)
                evac(norm_no("F2", NC - 1), SIDE_LAST)
                for p in range(NP):
                    silu(ffn_no("F2", NC - 1), norm_no("F2", NC - 1), p, SIDE_LAST)

            @block.tensor
            def _(pe):
                T_ = nc.tensor

                def chain(dst, terms):
                    for n, (lhsT, rhs) in enumerate(terms):
                        last = T_.matmul(dst, lhsT, rhs, start=(n == 0), stop=(n == len(terms) - 1))
                    return last

                def turn(L, side):
                    pe.wait_ge(n_done, TT * (L + 1))
                    for k in range(KH):
                        for t in range(TT):
                            last = T_.transpose(W[side][:, k, t * P:(t + 1) * P], nrm[:, t, k * P:(k + 1) * P], ident[:])
                    last.then_inc(n_tr, 1)

                def ffn(F, L, side, free, then=None):
                    for p in range(NP):
                        Wp = W[(side + p) % 2]
                        if p == 0:
                            pe.wait_ge(n_T, L + 1)
                        elif p == 1 and free:
                            pe.wait_ge(*free)
                        elif p > 1:
                            pe.wait_ge(f_h, NP * F + p - 1)
                        for half, wt in ((0, wg), (2, wu)):
                            for m, r in rows(p):
                                last = chain(Wp[0:r, half + m % 2, :], [(wt[:, k, m * P:m * P + r], nT[:, k, :]) for k in range(KH)])
                        last.then_inc(f_gu, 1)
                    pe.wait_ge(f_h, NP * F + NP - 1)
                    o = W[side][:].rearrange("p (t a) n -> p t (a n)", t=TT)

                    def down(t, k):
                        r = LAST if k == MI - 1 else P
                        return T_.matmul(o[:, t, :], hT[0:r, k, t * P:(t + 1) * P], wd[0:r, k, :], start=(k == 0), stop=(k == MI - 1))

                    for k in range(MI - 1):
                        down(0, k)
                    pe.wait_ge(f_h, NP * F + NP)
                    down(0, MI - 1)
                    for k in range(MI):
                        if k == TURN_AT and then is not None:
                            turn(then, 1 - side)
                        last = down(1, k)
                    last.then_inc(f_out, 1)

                def project(i, t, k0=0, k1=ME):
                    pe.wait_ge(m_y, 2 * (i + 1))
                    o = W[1][:].rearrange("p (t a) n -> p t (a n)", t=TT)
                    for k in range(k0, k1):
                        last = T_.matmul(o[:, t, :], sgm[:, k, t * P:(t + 1) * P], wo[:, k, :], start=(k == 0), stop=(k == ME - 1))
                    if k1 == ME:
                        last.then_inc(m_out, 1)

                def first_product(i, free, h_free):
                    pe.wait_ge(n_T, norm_no("M", i) + 1)
                    for h in range(2):
                        if h == h_free:
                            pe.wait_ge(*free)
                        for m in range(4 * h, 4 * h + 4):
                            last = chain(W[h][:, m % 4, :], [(win[:, k, m * P:(m + 1) * P], nT[:, k, :]) for k in range(KH)])
                        last.then_inc(m_x, 1)

                def step(i, back, f1, more):
                    for q in range(ME // 2):
                        if back and q == 2:
                            pe.wait_ge(m_tap, ME * (i + 1))
                            project(i - 1, 0, 0, FILL)
                        pe.wait_ge(m_u, 4 * i + q + 1)
                        for k in (2 * q, 2 * q + 1):
                            dt = T_.matmul(W[0][:, 0, :], wx[:, k, 0:R], U[:, k, :], start=(k == 0), stop=(k == ME - 1))
                        if q == ME // 2 - 1:
                            dt.then_inc(m_dt, 1)
                        for k in (2 * q, 2 * q + 1):
                            bc = T_.matmul(W[0][0:2 * S, 2, :], wx[:, k, R:R + 2 * S], U[:, k, :], start=(k == 0), stop=(k == ME - 1))
                    bc.then_inc(m_bc, 1)
                    pe.wait_ge(s_prod, NE * i)
                    pe.wait_ge(m_dtl, i + 1)
                    for m in range(ME):
                        last = chain(D[:, m, :], [(wdt[:, m * P:(m + 1) * P], dtl[:])])
                        if m % 2:
                            last.then_inc(m_dp, 1)
                    if back:
                        project(i - 1, 0, FILL)
                        project(i - 1, 1)
                    pe.wait_ge(m_bcS, i + 1)
                    for h in range(2):
                        if h == 1:
                            pe.wait_ge(m_res, i)
                        for m in range(4 * h, 4 * h + 4):
                            last = chain(W[h][:, m % 4, :], [(win[:, k, E + m * P:E + (m + 1) * P], nT[:, k, :]) for k in range(KH)])
                        last.then_inc(m_g, 1)
                    mamba = norm_no("M", i + 1) if more else None
                    F, L = ffn_no(*late(i)), norm_no(*late(i))
                    pe.wait_ge(m_sg, 2 * i + 1)
                    if f1:
                        E_, L_ = ffn_no(*early(i)), norm_no(*early(i))
                        turn(L_, SIDE_EARLY)
                        ffn(E_, L_, SIDE_EARLY, (m_sg, 2 * i + 2), L)
                        ffn(F, L, 1 - SIDE_EARLY, (f_res, E_ + 1), mamba)
                    else:
                        turn(L, SIDE_EARLY)
                        ffn(F, L, SIDE_EARLY, (m_sg, 2 * i + 2), mamba)
                    if more:
                        first_product(i + 1, (f_res, F + 1), side_late(f1))

                turn(0, SIDE_0)
                ffn(0, 0, SIDE_0, None)
                turn(1, 1 - SIDE_0)
                pe.wait_ge(wts_loaded, 64)
                first_product(0, (f_res, 1), SIDE_0)
                steps_b(step, pe)
                F = ffn_no("F2", NC - 2)
                pe.wait_ge(f_h, NP * (F + 1))
                for t in range(TT):
                    project(NC - 1, t)
                pe.wait_ge(f_res, F + 1)
                turn(norm_no("F2", NC - 1), SIDE_LAST)
                ffn(F + 1, norm_no("F2", NC - 1), SIDE_LAST, (m_res, NC))

            @block.vector
            def _(dve):
                V = nc.vector

                def alone(semaphore, count):
                    dve.wait_ge(semaphore, count)
                    V.memset(tick[:], 0.0)

                def stats(L, rows_):
                    dve.wait_ge(n_done, TT * L)
                    for t in range(TT):
                        V.bn_stats(bnst[:, t, :], rows_[:, t, :]).then_inc(n_stat, 1)
                    alone(n_stat, TT * (L + 1))
                    for t in range(TT):
                        V.bn_aggr(mv[:, t, :], bnst[:, t, :]).then_inc(n_var, 1)
                    dve.wait_ge(n_var, TT * (L + 1))
                    V.tensor_scalar(veps[:], mv[:, :, 1], EPS, None, ALU.add).then_inc(n_veps, 1)

                def norm(L, rows_):
                    dve.wait_ge(n_rstd, L + 1)
                    for t in range(TT):
                        V.tensor_scalar(nrm[:, t, :], rows_[:, t, :], mv[:, t, 0:1], rstd[:, t:t + 1],
                                        ALU.subtract, ALU.mult).then_inc(n_done, 1)

                def gated(F, p, side):
                    dve.wait_ge(f_silu, NP * F + p + 1)
                    if p == 0:
                        dve.wait_ge(f_out, F)
                    r = rows(p)
                    n, w = r[0][1], len(r)
                    V.tensor_tensor(hT[0:n, 2 * p:2 * p + w, :], nrm[0:n, p % 2, 0:w * CH].rearrange("p (a t) -> p a t", a=w),
                                    W[(side + p) % 2][0:n, 2:2 + w, :], ALU.mult).then_inc(f_h, 1)

                def resid(ready, count, rows_, done, side):
                    dve.wait_ge(ready, count)
                    V.tensor_tensor(rows_[:].rearrange("p t d -> p (t d)"), W[side][:].rearrange("p a n -> p (a n)"),
                                    rows_[:].rearrange("p t d -> p (t d)"), ALU.add).then_inc(done, 1)

                def gate_y(i):
                    dve.wait_ge(s_acc, pool_sums(i + 1))
                    dve.wait_ge(s_prod, NE * (i + 1))
                    dve.wait_ge(m_sg, 2 * (i + 1))
                    for h in range(2):
                        g = sgm[:, 4 * h:4 * h + 4, :]
                        V.tensor_tensor(g, yacc[:, 4 * h:4 * h + 4, :], g, ALU.mult).then_inc(m_y, 1)

                def out_resid(i):
                    dve.wait_ge(x3_loaded, 16 * (i + 2))
                    resid(m_out, TT * (i + 1), X3, m_res, 1)

                def conv(i, q):
                    x_ = xext[q % 2]
                    cq = cc[:, 2 * q:2 * q + 2, :]
                    dve.wait_ge(m_conv, 24 * i + 6 * max(q - 1, 0))
                    dve.wait_ge(m_cc, 4 * i + max(q - 1, 0))
                    V.tensor_copy(x_[:, :, 0:KC - 1], cq).then_inc(m_in, 1)
                    dve.wait_ge(m_tap, ME * i + 2 * q + 2)
                    dve.wait_ge(m_in, 4 * i + q + 1)
                    for k in range(KC - 1):
                        for h in range(2):
                            m = 2 * q + h
                            if k:
                                dve.wait_ge(m_conv, 24 * i + 6 * q + 2 * (k - 1) + h + 1)
                            V.scalar_tensor_tensor(U[:, m, :], x_[:, h, k:k + CH], cw[:, m, k:k + 1], U[:, m, :],
                                                   ALU.mult, ALU.add).then_inc(m_conv, 1)
                    V.tensor_scalar(cq, x_[:, :, CH:CH + KC - 1], keep[:, bass.ds(i + 1, 1)], None, ALU.mult).then_inc(m_cc, 1)

                def step(i, back, f1, more):
                    at = places(f1)
                    for q in range(ME // 2):
                        conv(i, q)
                    if f1:
                        if back:
                            dve.wait_ge(xm_loaded, 16 * (load_no("x1", i + 2) + 1))
                        else:
                            dve.wait_ge(x3_loaded, 16)
                        early_rows = XM if back else X3
                        stats(norm_no(*early(i)), early_rows)
                        dve.wait_ge(n_tr, norm_no("M", i) + 1)
                        norm(norm_no(*early(i)), early_rows)
                    dve.wait_ge(s_dA, 2 * NE * i)
                    for m in range(ME):
                        dve.wait_ge(m_abs, ME * i + m + 2 - m % 2)
                        V.tensor_scalar(delta[:, m, :], D[:, m, :], bdt[:, m:m + 1], 0.0, ALU.add, ALU.max).then_inc(m_relu, 1)
                    for j in range(ME // 2):
                        pair = slice(2 * j, 2 * j + 2)
                        dve.wait_ge(m_ln, 4 * i + j + 1)
                        dve.wait_ge(m_relu, ME * i + 2 * (j + 1))
                        V.tensor_tensor(delta[:, pair, :], delta[:, pair, :], dBu[j][:], ALU.add).then_inc(m_delta, 1)
                        dve.wait_ge(m_skip, ME * (i + 1))
                        dve.wait_ge(m_bc, i + 1)
                        dve.wait_ge(m_delta, 4 * i + j + 1)
                        V.tensor_tensor(U[:, pair, :], U[:, pair, :], delta[:, pair, :], ALU.mult).then_inc(m_du, 1)

                    if back:
                        out_resid(i - 1)

                    def scan(e, m):
                        dve.wait_ge(s_dA, 2 * NE * i + 2 * e + 2)
                        dve.wait_ge(s_dBu, NE * i + e + 1)
                        dve.wait_ge(s_hc, NE * i)
                        n = e // 4
                        V.tensor_tensor_scan(D[:, m, :], D[:, m, :], dBu[e % 4][:, m % 2, :], hc[:, n, m:m + 1],
                                             ALU.mult, ALU.add).then_inc(s_scan, 1)

                    def save(e):
                        n, j = divmod(e, 4)
                        dve.wait_ge(s_scan, 2 * NE * i + 2 * e + 2)
                        V.tensor_scalar(hc[:, n, 2 * j:2 * j + 2], D[:, 2 * j:2 * j + 2, CH - 1], keep[:, bass.ds(i + 1, 1)], None,
                                        ALU.mult).then_inc(s_hc, 1)

                    def times_c(e):
                        n, j = divmod(e, 4)
                        h_, r = D[:, 2 * j:2 * j + 2, :], pool_pairs(f1) * n + j
                        c_ = BC[n % 3][:, 1:2, :].to_broadcast([P, 2, CH])
                        dve.wait_ge(bc_loaded[n % 3], 16 * ((6 if n % 3 == 0 else 5) * i + n // 3 + 1))
                        if j < pool_pairs(f1):
                            dve.wait_ge(s_acc, pool_sums(i) + max(r - 1, 0))
                            V.tensor_tensor(prod[r % 2][:], h_, c_, ALU.mult).then_inc(s_prod, 1)
                        else:
                            dve.wait_ge(s_hc, NE * i + e + 1)
                            V.tensor_tensor(h_, h_, c_, ALU.mult).then_inc(s_hC, 1)

                    def add(e):
                        n, j = divmod(e, 4)
                        pair, mine = slice(2 * j, 2 * j + 2), 4 - pool_pairs(f1)
                        dve.wait_ge(m_skip, ME * (i + 1))
                        dve.wait_ge(s_prod, NE * i + e - 3)
                        dve.wait_ge(s_hC, dve_sums(i) + mine * n + j - pool_pairs(f1) + 1)
                        V.tensor_tensor(yacc[:, pair, :], D[:, pair, :], yacc[:, pair, :], ALU.add).then_inc(s_prod, 1)

                    for e in range(NE + 4):
                        j = e % 4
                        if e < NE:
                            scan(e, 2 * j)
                        if 1 <= e <= NE:
                            save(e - 1)
                        if e < NE:
                            scan(e, 2 * j + 1)
                        if 2 <= e <= NE + 1 and (e - 2) % 4 >= pool_pairs(f1):
                            add(e - 2)
                        if 1 <= e <= NE:
                            times_c(e - 1)
                        if e == NE + 1:
                            gate_y(i)
                        late_rows = X3 if back else XM
                        if e == F2_STAT:
                            if back:
                                dve.wait_ge(m_res, i)
                            else:
                                dve.wait_ge(xm_loaded, 16 * (load_no("x1", 2) + 1))
                            stats(norm_no(*late(i)), late_rows)
                        if e == at["norm"]:
                            if f1:
                                dve.wait_ge(f_h, NP * (ffn_no(*early(i)) + 1))
                            else:
                                dve.wait_ge(n_tr, norm_no("M", i) + 1)
                            norm(norm_no(*late(i)), late_rows)
                        for p in range(NP):
                            if f1 and e == F1_SILU[p] + MULT:
                                gated(ffn_no(*early(i)), p, SIDE_EARLY)
                            if e == at["silu"][p] + MULT:
                                gated(ffn_no(*late(i)), p, side_late(f1))
                        if f1 and e == F1_RES:
                            resid(f_out, ffn_no(*early(i)) + 1, early_rows, f_res, SIDE_EARLY)
                        if e == at["res"]:
                            resid(f_out, ffn_no(*late(i)) + 1, late_rows, f_res, side_late(f1))
                        if more and e == at["m_stat"]:
                            if back:
                                dve.wait_ge(xm_loaded, 16 * (load_no("x2", i + 1) + 1))
                            else:
                                dve.wait_ge(f_res, ffn_no(*early(i)) + 1)
                            stats(norm_no("M", i + 1), XM if back else X3)
                        if more and e == at["m_norm"]:
                            dve.wait_ge(f_h, NP * (ffn_no(*late(i)) + 1))
                            norm(norm_no("M", i + 1), XM if back else X3)

                V.memset(hc[:], 0.0)
                V.memset(cc[:], 0.0).then_inc(b_setup, 1)
                dve.wait_ge(b_setup, 2)
                V.tensor_scalar(A[:], A[:], -1.0, None, ALU.mult).then_inc(b_setup, 1)
                dve.wait_ge(xm_loaded, 16)
                stats(0, XM)
                norm(0, XM)
                for p in range(NP):
                    gated(0, p, SIDE_0)
                resid(f_out, 1, XM, f_res, SIDE_0)
                dve.wait_ge(f_h, NP)
                dve.wait_ge(f_res, 1)
                stats(1, XM)
                norm(1, XM)
                steps_b(step, dve)
                out_resid(NC - 1)
                L, F = norm_no("F2", NC - 1), ffn_no("F2", NC - 1)
                dve.wait_ge(m_res, NC)
                dve.wait_ge(f_h, NP * F)
                stats(L, X3)
                norm(L, X3)
                for p in range(NP):
                    gated(F, p, SIDE_LAST)
                resid(f_out, F + 1, X3, f_res, SIDE_LAST)
    return nc


def kernel(**a):
    import numpy as np
    import concourse.bacc as bacc
    from concourse.bass_utils import run_bass_kernel_spmd

    ffn, mamba, rwkv = "L0_ffn_", "L0_attn_b_", "L0_attn_a_"
    x = np.asarray(a[rwkv + "x"])
    B, T, H = x.shape

    def columns(v):
        v = np.asarray(v)
        return np.moveaxis(v.reshape((-1, P) + v.shape[1:]), 0, 1)

    gate, up, down = (np.asarray(a[ffn + n]) for n in ("gate_idx", "up_idx", "down_idx"))
    inner = gate.shape[0]
    tiles = -(-inner // P)
    down = np.pad(down.T, ((0, tiles * P - inner), (0, 0)))
    idx = np.concatenate([columns(w).reshape(P, -1) for w in (gate.T, up.T, down)], axis=1)
    arrays = dict(
        x=x.reshape(B * T, H),
        w_rvk=np.asarray(a[rwkv + "W_rvk"]).T,
        w_out=np.asarray(a[rwkv + "W_out"]).T,
        decay=columns(a[rwkv + "time_decay"]),
        first=columns(a[rwkv + "time_first"]),
        idx=idx,
        lut=np.asarray(a[ffn + "lut"]),
        w_in=np.asarray(a[mamba + "in_proj_w"]).T,
        conv_w=columns(np.asarray(a[mamba + "conv_w"])[:, 0]),
        conv_b=columns(a[mamba + "conv_b"]),
        w_x=np.asarray(a[mamba + "x_proj_w"]).T,
        w_dt=np.asarray(a[mamba + "dt_proj_w"]).T,
        b_dt=columns(a[mamba + "dt_proj_b"]),
        a_log=columns(a[mamba + "A_log"]),
        d_skip=columns(a[mamba + "D_param"]),
        w_o=np.asarray(a[mamba + "out_proj_w"]).T,
    )
    arrays = {n: np.ascontiguousarray(v) for n, v in arrays.items()}
    nc = bacc.Bacc("TRN2", target_bir_lowering=False, num_devices=1)
    args = {n: nc.dram_tensor(n, v.shape, mybir.dt.from_np(v.dtype), kind="ExternalInput").ap() for n, v in arrays.items()}
    out = nc.dram_tensor("out", (B * T, H), F32, kind="ExternalOutput").ap()
    hybrid_block_kernel(nc, **args, inner=inner, out=out)
    r = run_bass_kernel_spmd(nc, [arrays], core_ids=[0])
    return np.asarray(r.results[0]["out"]).reshape(B, T, H)
```
